# Optimizing a Trainium2 kernel written in Bass

```python
import numpy as np
import jax
import jax.numpy as jnp

def _softmax(x, axis=-1):
    return jax.nn.softmax(x, axis=axis)

def _gelu(x):
    return jax.nn.gelu(x, approximate=True)

def _silu(x):
    return jax.nn.silu(x)

def _sigmoid(x):
    return jax.nn.sigmoid(x)

def _layernorm(x, axis=-1, eps=1e-05):
    m = jnp.mean(x, axis=axis, keepdims=True)
    v = jnp.var(x, axis=axis, keepdims=True)
    return (x - m) / jnp.sqrt(v + eps)

def _scatter_add(tgt, idx, src, axis=0):
    return tgt.at[idx].add(src)

def _segment_sum(src, seg, n):
    return jax.ops.segment_sum(src, seg, n)
kernel_name = 'mk_decoder_preln_d1_seqx_r2_47ac77'

def setup_inputs(seed: int=0):
    np.random.seed(seed)
    _w = jnp.asarray

    def _rec_inputs():
        import jax
        import jax.numpy as jnp
        _rk = jax.random.key(seed)
        x = -0.0002928 + 1 * jax.random.normal(jax.random.fold_in(_rk, 1), (16, 224, 512), jnp.float32)
        _lenS = 224 - jax.random.randint(jax.random.fold_in(_rk, 7), (16,), 0, max(1, 224 // 4) + 1, jnp.int32)
        _lenS2 = 750 - jax.random.randint(jax.random.fold_in(_rk, 8), (16,), 0, max(1, 750 // 4) + 1, jnp.int32)
        _ctx_1024P = jax.random.normal(jax.random.fold_in(_rk, 11), (16, 16, 512), jnp.float32)
        _ctx_1024c = jax.random.dirichlet(jax.random.fold_in(_rk, 511), 0.3 * jnp.ones((16,), jnp.float32), (16, 750))
        _ctx_1024t = jnp.einsum('bsk,bkd->bsd', _ctx_1024c, _ctx_1024P)
        _ctx_1024t = _ctx_1024t * jax.lax.rsqrt(jnp.mean(jnp.square(_ctx_1024t)) + 1e-12) * 0.953939
        ctx_1024 = 0.000376506 + 0.999991 * (_ctx_1024t + 0.3 * jax.random.normal(jax.random.fold_in(_rk, 611), (16, 750, 512), jnp.float32))
        _validS = jnp.arange(224)[None, :] < _lenS[:, None]
        _validS2 = jnp.arange(750)[None, :] < _lenS2[:, None]
        _causal = jnp.tril(jnp.ones((224, 224), dtype=bool))
        mask_1x1xSxS2_fk1 = jnp.where(jnp.broadcast_to(_validS2[0:1, None, None, :], (1, 1, 224, 750)), 1.0, 0.0).astype(jnp.float32)
        return (x, ctx_1024, mask_1x1xSxS2_fk1)
    x, ctx_1024, mask_1x1xSxS2_fk1 = _rec_inputs()

    def _L0_attn_setup():
        import jax, jax.numpy as jnp
        import numpy as np
        D_MODEL, D_INNER, D_STATE, D_CONV, DT_RANK = (512, 1024, 16, 4, 64)
        EPS = 1e-05

        def _rmsnorm(x, w):
            x = x.astype(jnp.float32)
            return x * jax.lax.rsqrt(jnp.mean(x * x, axis=-1, keepdims=True) + EPS) * w

        def _mamba_block(residual, norm_w, W_in, conv_w, conv_b, W_x, W_dt, b_dt, A_log, D, W_out):
            B, L, _ = residual.shape
            hidden = _rmsnorm(residual, norm_w)
            residual = residual.astype(jnp.float32)
            xz = hidden @ W_in
            x, z = jnp.split(xz, 2, axis=-1)
            xc = jax.lax.conv_general_dilated(x.transpose(0, 2, 1), conv_w[:, None, :], (1,), [(D_CONV - 1, 0)], dimension_numbers=('NCH', 'OIH', 'NCH'), feature_group_count=D_INNER)
            x = jax.nn.silu((xc + conv_b[None, :, None]).transpose(0, 2, 1))
            x_dbl = x @ W_x
            dt = jax.nn.softplus(x_dbl[..., :DT_RANK] @ W_dt + b_dt)
            Bm = x_dbl[..., DT_RANK:DT_RANK + D_STATE]
            Cm = x_dbl[..., DT_RANK + D_STATE:]
            A = -jnp.exp(A_log)

            def step(h, inp):
                x_t, dt_t, B_t, C_t = inp
                dA = jnp.exp(dt_t[..., None] * A)
                h = dA * h + (dt_t * x_t)[..., None] * B_t[:, None, :]
                y = jnp.einsum('bdn,bn->bd', h, C_t)
                return (h, y)
            h0 = jnp.zeros((B, D_INNER, D_STATE), jnp.float32)
            xs = (x.transpose(1, 0, 2), dt.transpose(1, 0, 2), Bm.transpose(1, 0, 2), Cm.transpose(1, 0, 2))
            _, ys = jax.lax.scan(step, h0, xs)
            y = ys.transpose(1, 0, 2) + x * D
            y = y * jax.nn.silu(z)
            out = y @ W_out
            return residual + out
        key = jax.random.key(seed)
        ks = jax.random.split(key, 10)
        s = 0.02
        residual = jax.random.normal(ks[0], (2, 1024, D_MODEL), dtype=jnp.float32)
        norm_w = jnp.ones((D_MODEL,), jnp.float32)
        W_in = jax.random.normal(ks[1], (D_MODEL, 2 * D_INNER), jnp.float32) * s
        conv_w = jax.random.normal(ks[2], (D_INNER, D_CONV), jnp.float32) * s
        conv_b = jnp.zeros((D_INNER,), jnp.float32)
        W_x = jax.random.normal(ks[3], (D_INNER, DT_RANK + 2 * D_STATE), jnp.float32) * s
        W_dt = jax.random.normal(ks[4], (DT_RANK, D_INNER), jnp.float32) * s
        b_dt = jax.random.uniform(ks[5], (D_INNER,), jnp.float32, -4.0, -2.0)
        A_log = jnp.log(jnp.broadcast_to(jnp.arange(1, D_STATE + 1, dtype=jnp.float32), (D_INNER, D_STATE)))
        D = jnp.ones((D_INNER,), jnp.float32)
        W_out = jax.random.normal(ks[6], (D_INNER, D_MODEL), jnp.float32) * s
        return dict(residual=residual, norm_w=norm_w, W_in=W_in, conv_w=conv_w, conv_b=conv_b, W_x=W_x, W_dt=W_dt, b_dt=b_dt, A_log=A_log, D=D, W_out=W_out)
    _L0_attn_all = _L0_attn_setup()
    _L0_attn_in = {k: v for k, v in _L0_attn_all.items() if k in ('norm_w', 'W_in', 'conv_w', 'conv_b', 'W_x', 'W_dt', 'b_dt', 'A_log', 'D', 'W_out')}
    del _L0_attn_all

    def _L0_xattn_setup():
        import jax, jax.numpy as jnp
        import numpy as np
        D_MODEL = 512
        NUM_HEADS = 16
        DEPTH = D_MODEL // NUM_HEADS
        NEG_INF_SCALE = -1000000000.0

        def _split_heads(x):
            B, S, _ = x.shape
            return x.reshape(B, S, NUM_HEADS, DEPTH).transpose(0, 2, 1, 3)
        key = jax.random.key(seed)
        ks = jax.random.split(key, 12)
        B, S = (2, 1024)
        q = jax.random.normal(ks[0], (B, S, D_MODEL), dtype=jnp.float32)
        k = jax.random.normal(ks[1], (B, S, D_MODEL), dtype=jnp.float32)
        v = jax.random.normal(ks[2], (B, S, D_MODEL), dtype=jnp.float32)
        mask = jnp.triu(jnp.ones((S, S), dtype=jnp.float32), k=1)[None, None]
        scale = 1.0 / np.sqrt(D_MODEL)
        Wq = jax.random.normal(ks[3], (D_MODEL, D_MODEL), dtype=jnp.float32) * scale
        bq = jnp.zeros((D_MODEL,), dtype=jnp.float32)
        Wk = jax.random.normal(ks[4], (D_MODEL, D_MODEL), dtype=jnp.float32) * scale
        bk = jnp.zeros((D_MODEL,), dtype=jnp.float32)
        Wv = jax.random.normal(ks[5], (D_MODEL, D_MODEL), dtype=jnp.float32) * scale
        bv = jnp.zeros((D_MODEL,), dtype=jnp.float32)
        Wo = jax.random.normal(ks[6], (D_MODEL, D_MODEL), dtype=jnp.float32) * scale
        bo = jnp.zeros((D_MODEL,), dtype=jnp.float32)
        return {'v': v, 'k': k, 'q': q, 'mask': mask, 'Wq': Wq, 'bq': bq, 'Wk': Wk, 'bk': bk, 'Wv': Wv, 'bv': bv, 'Wo': Wo, 'bo': bo}
    _L0_xattn_all = _L0_xattn_setup()
    _L0_xattn_in = {k: v for k, v in _L0_xattn_all.items() if k in ('Wq', 'bq', 'Wk', 'bk', 'Wv', 'bv', 'Wo', 'bo')}
    del _L0_xattn_all

    def _L0_ffn_setup():
        import jax, jax.numpy as jnp
        import numpy as np

        def _binarize(w):
            alpha = jax.lax.stop_gradient(jnp.mean(jnp.abs(w), axis=1, keepdims=True))
            bw = alpha * jnp.sign(w)
            return w + jax.lax.stop_gradient(bw - w)
        key = jax.random.key(seed)
        k1, k2, k3, k4, k5 = jax.random.split(key, 5)
        D, H = (512, 2048)
        x = jax.random.normal(k1, (64, 196, D), dtype=jnp.float32)
        w1 = jax.random.normal(k2, (H, D), dtype=jnp.float32) * 0.02
        b1 = jax.random.normal(k3, (H,), dtype=jnp.float32) * 0.02
        w2 = jax.random.normal(k4, (D, H), dtype=jnp.float32) * 0.02
        b2 = jax.random.normal(k5, (D,), dtype=jnp.float32) * 0.02
        return {'x': x, 'w1': w1, 'b1': b1, 'w2': w2, 'b2': b2}
    _L0_ffn_all = _L0_ffn_setup()
    _L0_ffn_in = {k: v for k, v in _L0_ffn_all.items() if k in ('w1', 'b1', 'w2', 'b2')}
    del _L0_ffn_all
    return {'x': x, 'ctx_1024': ctx_1024, 'mask_1x1xSxS2_fk1': mask_1x1xSxS2_fk1, 'L0_attn_norm_w': _L0_attn_in['norm_w'], 'L0_attn_W_in': _L0_attn_in['W_in'], 'L0_attn_conv_w': _L0_attn_in['conv_w'], 'L0_attn_conv_b': _L0_attn_in['conv_b'], 'L0_attn_W_x': _L0_attn_in['W_x'], 'L0_attn_W_dt': _L0_attn_in['W_dt'], 'L0_attn_b_dt': _L0_attn_in['b_dt'], 'L0_attn_A_log': _L0_attn_in['A_log'], 'L0_attn_D': _L0_attn_in['D'], 'L0_attn_W_out': _L0_attn_in['W_out'], 'L0_xattn_Wq': _L0_xattn_in['Wq'], 'L0_xattn_bq': _L0_xattn_in['bq'], 'L0_xattn_Wk': _L0_xattn_in['Wk'], 'L0_xattn_bk': _L0_xattn_in['bk'], 'L0_xattn_Wv': _L0_xattn_in['Wv'], 'L0_xattn_bv': _L0_xattn_in['bv'], 'L0_xattn_Wo': _L0_xattn_in['Wo'], 'L0_xattn_bo': _L0_xattn_in['bo'], 'L0_ffn_w1': _L0_ffn_in['w1'], 'L0_ffn_b1': _L0_ffn_in['b1'], 'L0_ffn_w2': _L0_ffn_in['w2'], 'L0_ffn_b2': _L0_ffn_in['b2']}

def reference(x, ctx_1024, mask_1x1xSxS2_fk1, L0_attn_norm_w, L0_attn_W_in, L0_attn_conv_w, L0_attn_conv_b, L0_attn_W_x, L0_attn_W_dt, L0_attn_b_dt, L0_attn_A_log, L0_attn_D, L0_attn_W_out, L0_xattn_Wq, L0_xattn_bq, L0_xattn_Wk, L0_xattn_bk, L0_xattn_Wv, L0_xattn_bv, L0_xattn_Wo, L0_xattn_bo, L0_ffn_w1, L0_ffn_b1, L0_ffn_w2, L0_ffn_b2):
    import jax
    import jax.numpy as jnp

    def _L0_attn_ref(residual, norm_w, W_in, conv_w, conv_b, W_x, W_dt, b_dt, A_log, D, W_out):
        import jax, jax.numpy as jnp
        import numpy as np
        D_MODEL, D_INNER, D_STATE, D_CONV, DT_RANK = (512, 1024, 16, 4, 64)
        EPS = 1e-05

        def _rmsnorm(x, w):
            x = x.astype(jnp.float32)
            return x * jax.lax.rsqrt(jnp.mean(x * x, axis=-1, keepdims=True) + EPS) * w

        def _mamba_block(residual, norm_w, W_in, conv_w, conv_b, W_x, W_dt, b_dt, A_log, D, W_out):
            B, L, _ = residual.shape
            hidden = _rmsnorm(residual, norm_w)
            residual = residual.astype(jnp.float32)
            xz = hidden @ W_in
            x, z = jnp.split(xz, 2, axis=-1)
            xc = jax.lax.conv_general_dilated(x.transpose(0, 2, 1), conv_w[:, None, :], (1,), [(D_CONV - 1, 0)], dimension_numbers=('NCH', 'OIH', 'NCH'), feature_group_count=D_INNER)
            x = jax.nn.silu((xc + conv_b[None, :, None]).transpose(0, 2, 1))
            x_dbl = x @ W_x
            dt = jax.nn.softplus(x_dbl[..., :DT_RANK] @ W_dt + b_dt)
            Bm = x_dbl[..., DT_RANK:DT_RANK + D_STATE]
            Cm = x_dbl[..., DT_RANK + D_STATE:]
            A = -jnp.exp(A_log)

            def step(h, inp):
                x_t, dt_t, B_t, C_t = inp
                dA = jnp.exp(dt_t[..., None] * A)
                h = dA * h + (dt_t * x_t)[..., None] * B_t[:, None, :]
                y = jnp.einsum('bdn,bn->bd', h, C_t)
                return (h, y)
            h0 = jnp.zeros((B, D_INNER, D_STATE), jnp.float32)
            xs = (x.transpose(1, 0, 2), dt.transpose(1, 0, 2), Bm.transpose(1, 0, 2), Cm.transpose(1, 0, 2))
            _, ys = jax.lax.scan(step, h0, xs)
            y = ys.transpose(1, 0, 2) + x * D
            y = y * jax.nn.silu(z)
            out = y @ W_out
            return residual + out
        return _mamba_block(residual, norm_w, W_in, conv_w, conv_b, W_x, W_dt, b_dt, A_log, D, W_out)

    def _L0_xattn_ref(v, k, q, mask, Wq, bq, Wk, bk, Wv, bv, Wo, bo):
        import jax, jax.numpy as jnp
        import numpy as np
        D_MODEL = 512
        NUM_HEADS = 16
        DEPTH = D_MODEL // NUM_HEADS
        NEG_INF_SCALE = -1000000000.0

        def _split_heads(x):
            B, S, _ = x.shape
            return x.reshape(B, S, NUM_HEADS, DEPTH).transpose(0, 2, 1, 3)
        B, Sq, _ = q.shape
        qh = _split_heads(q @ Wq + bq)
        kh = _split_heads(k @ Wk + bk)
        vh = _split_heads(v @ Wv + bv)
        logits = jnp.einsum('bhqd,bhkd->bhqk', qh, kh) / jnp.sqrt(jnp.asarray(DEPTH, dtype=jnp.float32))
        logits = logits + mask * NEG_INF_SCALE
        attn = jax.nn.softmax(logits, axis=-1)
        out = jnp.einsum('bhqk,bhkd->bhqd', attn, vh)
        out = out.transpose(0, 2, 1, 3).reshape(B, Sq, D_MODEL)
        return out @ Wo + bo

    def _L0_ffn_ref(x, w1, b1, w2, b2):
        import jax, jax.numpy as jnp
        import numpy as np

        def _binarize(w):
            alpha = jax.lax.stop_gradient(jnp.mean(jnp.abs(w), axis=1, keepdims=True))
            bw = alpha * jnp.sign(w)
            return w + jax.lax.stop_gradient(bw - w)
        bw1 = _binarize(w1)
        h = jnp.einsum('bsd,hd->bsh', x, bw1) + b1
        h = jax.nn.gelu(h, approximate=False)
        bw2 = _binarize(w2)
        out = jnp.einsum('bsh,dh->bsd', h, bw2) + b2
        return out
    x = x + _L0_attn_ref(_layernorm(x, axis=-1), L0_attn_norm_w, L0_attn_W_in, L0_attn_conv_w, L0_attn_conv_b, L0_attn_W_x, L0_attn_W_dt, L0_attn_b_dt, L0_attn_A_log, L0_attn_D, L0_attn_W_out)
    x = x + _L0_xattn_ref(ctx_1024, ctx_1024, _layernorm(x, axis=-1), mask_1x1xSxS2_fk1, L0_xattn_Wq, L0_xattn_bq, L0_xattn_Wk, L0_xattn_bk, L0_xattn_Wv, L0_xattn_bv, L0_xattn_Wo, L0_xattn_bo)
    x = x + _L0_ffn_ref(_layernorm(x, axis=-1), L0_ffn_w1, L0_ffn_b1, L0_ffn_w2, L0_ffn_b2)
    return x

_drawn_inputs = setup_inputs


def setup_inputs(seed=0):
    import zlib

    import numpy as np

    out = dict(_drawn_inputs(seed))
    spreads = {'L0_attn_norm_w': (1.0, 0.6),
     'L0_attn_conv_b': (0.0, 0.8),
     'L0_attn_D': (1.0, 0.6),
     'L0_xattn_bq': (0.0, 2.0),
     'L0_xattn_bk': (0.0, 2.0),
     'L0_xattn_bv': (0.0, 2.0),
     'L0_xattn_bo': (0.0, 2.0)}
    factors = {'L0_attn_W_in': 8.0,
     'L0_attn_conv_w': 8.0,
     'L0_attn_W_x': 8.0,
     'L0_attn_W_dt': 8.0,
     'L0_attn_b_dt': 8.0,
     'L0_attn_A_log': 8.0,
     'L0_attn_W_out': 8.0,
     'L0_ffn_b1': 200.0,
     'L0_ffn_b2': 200.0,
     'ctx_1024': 8.0,
     'L0_xattn_Wq': 8.0,
     'L0_xattn_Wk': 8.0,
     'L0_xattn_Wv': 8.0,
     'L0_xattn_Wo': 8.0,
     'L0_ffn_w1': 64.0,
     'L0_ffn_w2': 58.293}
    for name, (base, spread) in spreads.items():
        noise = np.random.default_rng([zlib.crc32(name.encode()), seed]).standard_normal(out[name].shape)
        drawn = base * np.exp(spread * noise) if base else spread * noise
        out[name] = jnp.asarray(drawn.astype(out[name].dtype))
    for name, factor in factors.items():
        out[name] = (out[name] * factor).astype(out[name].dtype)
    return out
```

```python
from contextlib import ExitStack

import numpy as np

import concourse.bass as bass
from concourse import mybir

P = 128
F32 = mybir.dt.float32
F32R = mybir.dt.float32r
ALU = mybir.AluOpType
ACT = mybir.ActivationFunctionType
AX_X = mybir.AxisListType.X
BANK = 512
EPS = 1e-5
NEG_INF_SCALE = -1e9
LOG1P_SMALL = 2.0 ** -8


class Counted:

    def __init__(self, sem):
        self.sem, self.value = sem, 0

    def after(self, instruction, by=1):
        instruction.then_inc(self.sem, by)
        self.value += by
        return self.sem, self.value


def wait(engine, *events):
    for event in events:
        if event is not None:
            engine.wait_ge(*event)


class Memory:

    def __init__(self, nc, stack, prefix):
        self.nc, self.stack, self.prefix = nc, stack, prefix

    def sbuf(self, name, shape, dtype=F32):
        return self.stack.enter_context(self.nc.sbuf_tensor(self.prefix + name, shape, dtype))

    def psum(self, name, shape):
        return self.stack.enter_context(self.nc.psum_tensor(self.prefix + name, shape, F32))

    def semaphore(self, name):
        return Counted(self.stack.enter_context(self.nc.semaphore(self.prefix + name)))


def newton_rsqrt(dve, done, out, guess, value, tmp):
    wait(dve, done.after(dve.tensor_tensor(tmp, guess, guess, ALU.mult)))
    wait(dve, done.after(dve.tensor_tensor(tmp, tmp, value, ALU.mult)))
    wait(dve, done.after(dve.tensor_scalar(tmp, tmp, -0.5, 1.5, ALU.mult, ALU.add)))
    event = done.after(dve.tensor_tensor(out, tmp, guess, ALU.mult))
    wait(dve, event)
    return event


def mamba_phase(nc, t, x1_dram, bc_dram, mv1, wsum):
    B, L, D = t["x"].shape
    TT = L // 2
    KD = D // P
    DI = t["W_out"].shape[0]
    M = DI // P
    R = t["W_dt"].shape[0]
    N = t["A_log"].shape[1]
    Q = N // 4
    TAPS = t["conv_w"].shape[1]
    PAIRS = M // 2
    SLOTS = 4 * PAIRS
    assert TT <= P and 2 * L <= BANK and R + 2 * N <= P

    pe, act, dve, pool, sp = nc.tensor, nc.scalar, nc.vector, nc.gpsimd, nc.sync
    with ExitStack() as stack:
        mem = Memory(nc, stack, "a_")
        w_in = mem.sbuf("w_in", [P, KD, 2 * DI])
        w_out = mem.sbuf("w_out", [P, M, D])
        w_x = mem.sbuf("w_x", [P, M, R + 2 * N])
        w_dt = mem.sbuf("w_dt", [R, DI])
        a_neg = mem.sbuf("a_neg", [P, M, N])
        norm_w = mem.sbuf("norm_w", [P, KD])
        conv_w = mem.sbuf("conv_w", [P, M, TAPS])
        conv_b = mem.sbuf("conv_b", [P, M])
        b_dt = mem.sbuf("b_dt", [P, M])
        d_skip = mem.sbuf("d_skip", [P, M])
        ident = mem.sbuf("ident", [P, P])
        series_bias = mem.sbuf("series_bias", [P, 1])
        xt = [mem.sbuf(f"xt{i}", [TT, 2, D]) for i in range(3)]
        ln = mem.sbuf("ln", [TT, 2, D])
        stats = mem.sbuf("stats", [TT, 2, 6])
        mv = mem.sbuf("mv", [TT, 2, 2])
        var_eps = mem.sbuf("var_eps", [TT, 2])
        guess = mem.sbuf("guess", [TT, 2])
        logv = mem.sbuf("logv", [TT, 2])
        ntmp = mem.sbuf("ntmp", [TT, 2])
        rstd = mem.sbuf("rstd", [TT, 2])
        ssum = mem.sbuf("ssum", [TT, 2])
        stats1 = mem.sbuf("stats1", [TT, 2, 6])
        hT = mem.sbuf("hT", [P, KD, L])
        square = hT[0:TT].rearrange("p k l -> p (k l)")[:, 0:D]
        conv = mem.sbuf("conv", [P, M, L])
        soft = mem.sbuf("soft", [P, M, L])
        xs = [mem.sbuf(f"xs{i}", [P, M, L]) for i in range(2)]
        zs = [mem.sbuf(f"zs{i}", [P, M, L]) for i in range(2)]
        dt = [mem.sbuf(f"dt{i}", [P, M, L]) for i in range(2)]
        yT = [mem.sbuf(f"yT{i}", [P, M, L]) for i in range(2)]
        piece = [mem.sbuf(f"piece{i}", [P, D]) for i in range(2)]
        xd = mem.sbuf("xd", [R + 2 * N, L])
        bmat = [mem.sbuf(f"bmat{i}", [P, Q, L]) for i in range(2)]
        cmat = [mem.sbuf(f"cmat{i}", [P, Q, L]) for i in range(2)]
        dA = [mem.sbuf(f"dA{i}", [P, 2, Q, L]) for i in range(2)]
        hs = [mem.sbuf(f"hs{i}", [P, 2, Q, L]) for i in range(3)]
        wide = mem.psum("wide", [P, 4, BANK])
        narrow = mem.psum("narrow", [P, 2, BANK])
        yps = mem.psum("yps", [P, 2, BANK])

        S = {n: mem.semaphore(n) for n in (
            "w", "xin0", "xin1", "xin2", "xout0", "xout1", "xout2", "piece0", "piece1", "bcst", "bc0", "bc1",
            "const", "dve", "act", "pool", "hT_ps", "wide_ps", "xd_ps", "y_ps", "o_ps",
            "dA", "dbx", "u", "scan", "hc", "evac", "xs_done", "zs_done")}

        k_in = t["W_in"].rearrange("(k p) m -> p k m", p=P)
        for k in range(KD):
            S["w"].after(sp.dma_start(w_in[:, k, :], k_in[:, k, :]), 16)
        for dst, src in (
            (w_out[:], t["W_out"].rearrange("(m p) d -> p m d", p=P)),
            (w_x[:], t["W_x"].rearrange("(m p) r -> p m r", p=P)),
            (w_dt[:], t["W_dt"]),
            (a_neg[:], t["A_log"].rearrange("(m p) n -> p m n", p=P)),
            (norm_w[:], t["norm_w"]), (conv_w[:], t["conv_w"].rearrange("(m p) k -> p m k", p=P)),
            (conv_b[:], t["conv_b"]), (b_dt[:], t["b_dt"]), (d_skip[:], t["D"]), (ident[:], t["ident"]),
        ):
            weights = S["w"].after(act.dma_start(dst, src), 16)
        act.preload_act_table_set("natural_log_exp_and_others")
        wait(act, weights)
        e = S["act"].after(act.activation(a_neg[:], a_neg[:], ACT.Exp))
        wait(dve, e)
        S["const"].after(dve.tensor_scalar(a_neg[:], a_neg[:], -1.0, None, ALU.mult))
        S["const"].after(dve.memset(series_bias[:], -(3.0 ** 0.5) / 4.0))
        for i in range(2):
            consts = S["const"].after(dve.memset(dA[i][:, :, :, 0:1], 0.0))
        for engine in (pe, act, dve, pool):
            wait(engine, weights, consts)

        ev = {}

        def got(*key):
            assert key in ev or min(key[1:]) < 0, key
            return ev.get(key)

        def load_x(b):
            wait(sp, got("x1_stored", b - 3))
            ev["x", b] = S[f"xin{b % 3}"].after(
                sp.dma_start(xt[b % 3][:], t["x"][b].rearrange("(i p) d -> p i d", p=TT)), 16)

        def row_stats(b):
            wait(dve, got("x", b))
            for i in range(2):
                e = S["dve"].after(dve.bn_stats(stats[:, i, :], xt[b % 3][:, i, :]))
            wait(dve, e)
            for i in range(2):
                e = S["dve"].after(dve.bn_aggr(mv[:, i, :], stats[:, i, :]))
            wait(dve, e)
            ev["var", b] = S["dve"].after(dve.tensor_scalar(var_eps[:], mv[:, :, 1], EPS, None, ALU.add))

        def guess_rsqrt(b, what, src, scale):
            wait(act, got(what, b))
            e = S["act"].after(act.activation(logv[:], src, ACT.Ln, scale=scale))
            wait(act, e)
            ev["guess_" + what, b] = S["act"].after(act.activation(guess[:], logv[:], ACT.Exp, scale=-0.5))

        def normalise(b):
            wait(dve, got("guess_var", b))
            newton_rsqrt(dve, S["dve"], rstd[:], guess[:], var_eps[:], ntmp[:])
            wait(dve, got("hT_read", b - 1))
            for i in range(2):
                ev["ln", b] = S["dve"].after(dve.tensor_scalar(
                    ln[:, i, :], xt[b % 3][:, i, :], mv[:, i, 0:1], rstd[:, i:i + 1], ALU.subtract, ALU.mult))

        def mean_square(b):
            wait(act, got("ln", b), got("z_ps_all", b - 1))
            for i in range(2):
                e = S["act"].after(act.activation(square, ln[:, i, :], ACT.Square, accum_out=ssum[:, i:i + 1]))
                wait(act, e)
            ev["sumsq", b] = e
            wait(pool, got("ln", b))
            ev["res", b] = S["pool"].after(pool.tensor_tensor(xt[b % 3][:], xt[b % 3][:], ln[:], ALU.add))

        def mean_square_eps(b):
            wait(dve, got("sumsq", b))
            ev["ms", b] = S["dve"].after(dve.tensor_scalar(var_eps[:], ssum[:], 1.0 / D, EPS, ALU.mult, ALU.add))

        def rms(b):
            wait(dve, got("guess_ms", b))
            newton_rsqrt(dve, S["dve"], rstd[:], guess[:], var_eps[:], ntmp[:])
            wait(dve, got("res", b))
            for i in range(2):
                ev["rms", b] = S["dve"].after(dve.tensor_scalar(
                    ln[:, i, :], ln[:, i, :], rstd[:, i:i + 1], None, ALU.mult))

        def transpose_h(b):
            wait(pe, got("rms", b), got("x1", b - 3), got("xd", b - 1))
            for k in range(KD):
                for i in range(2):
                    col = (k % 2) * L + i * TT
                    e = S["hT_ps"].after(pe.transpose(
                        narrow[:, k // 2, col:col + TT], ln[:, i, k * P:(k + 1) * P], ident[0:TT, 0:TT]))
            ev["hT_ps", b] = ev["hT_read", b] = e

        def scale_hT(b):
            wait(act, got("hT_ps", b), got("z_ps_all", b - 1))
            for k in range(KD):
                ev["hT", b] = S["act"].after(act.activation(
                    hT[:, k, :], narrow[:, k // 2, (k % 2) * L:(k % 2 + 1) * L], ACT.Copy, scale=norm_w[:, k:k + 1]))

        def project(b, first, pairs, free, name):
            wait(pe, got("hT", b), *free)
            for pair in pairs:
                for j in range(2):
                    m = first + 2 * pair + j
                    for k in range(KD):
                        mm = pe.matmul(wide[:, pair, j * L:(j + 1) * L], w_in[:, k, m * P:(m + 1) * P],
                                       hT[:, k, :], start=(k == 0), stop=(k == KD - 1))
                ev[name, b, pair] = ev[name + "_all", b] = S["wide_ps"].after(mm)

        def last_tap(b, pair):
            wait(act, got("x_ps", b, pair), got("dt", b - 1))
            for j in range(2):
                m = 2 * pair + j
                e = S["act"].after(act.activation(conv[:, m, :], wide[:, pair, j * L:(j + 1) * L], ACT.Identity,
                                                  scale=conv_w[:, m, TAPS - 1:TAPS], bias=conv_b[:, m:m + 1]))
            ev["tap", b, pair] = e

        def older_taps(b, pair):
            wait(dve, got("tap", b, pair))
            for back in range(1, TAPS):
                for j in range(2):
                    m = 2 * pair + j
                    e = S["dve"].after(dve.scalar_tensor_tensor(
                        out=conv[:, m, back:], in0=wide[:, pair, j * L:(j + 1) * L - back],
                        scalar=conv_w[:, m, TAPS - 1 - back:TAPS - back], in1=conv[:, m, back:],
                        op0=ALU.mult, op1=ALU.add))
                wait(dve, e)
            ev["conv", b, pair] = e

        def silus(b):
            wait(act, *(got("conv", b, p) for p in range(4)), *(got("z_ps", b, p) for p in range(4)))
            wait(act, got("gated", b - 2))
            ev["xs", b] = S["xs_done"].after(act.activation(xs[b % 2][:], conv[:], ACT.Silu))
            for pair in range(4):
                ev["zs", b] = S["zs_done"].after(act.activation(
                    zs[b % 2][:, 2 * pair:2 * pair + 2, :],
                    wide[:, pair, 0:2 * L].rearrange("p (j l) -> p j l", j=2), ACT.Silu))
            act.preload_act_table_set("natural_log_exp_and_others")

        def x_dbl(b):
            wait(pe, got("xs", b), got("hT", b), got("x1", b - 2))
            for m in range(M):
                mm = pe.matmul(narrow[0:R + 2 * N, 0, 0:L], w_x[:, m, :], xs[b % 2][:, m, :],
                               start=(m == 0), stop=(m == M - 1))
            ev["xd_ps", b] = S["xd_ps"].after(mm)

        def keep_xd(b):
            wait(act, got("xd_ps", b), got("dt_ps_all", b - 1), got("bc_stored", b - 1))
            ev["xd", b] = S["act"].after(act.activation(xd[:], narrow[0:R + 2 * N, 0, 0:L], ACT.Copy))
            wait(sp, ev["xd", b])
            ev["bc_stored", b] = S["bcst"].after(sp.dma_start(bc_dram[b], xd[R:R + 2 * N, :]), 16)

        def spread_bc(b, q):
            wait(sp, got("bc_stored", b), got("hc", b * SLOTS + q * PAIRS - PAIRS - 1))
            for dst, row in ((bmat[q % 2], q * Q), (cmat[q % 2], N + q * Q)):
                src = bc_dram[b, row:row + Q, :].partition_broadcast(P)
                ev["bc", b, q] = S[f"bc{q % 2}"].after(sp.dma_start(dst[:], src), 16)

        def dt_raw(b):
            wait(pe, got("xd", b), got("zs", b))
            for pair in range(4):
                for j in range(2):
                    m = 2 * pair + j
                    mm = pe.matmul(wide[:, pair, j * L:(j + 1) * L], w_dt[:, m * P:(m + 1) * P], xd[0:R, :],
                                   start=True, stop=True)
                ev["dt_ps", b, pair] = S["wide_ps"].after(mm)
            ev["dt_ps_all", b] = ev["dt_ps", b, 3]

        def softplus_abs(b):
            for pair in range(PAIRS):
                wait(dve, got("dt_ps", b, pair), got("dA_all", b - 2), got("u", b - 2))
                for j in range(2):
                    m = 2 * pair + j
                    ev["relu", b] = S["dve"].after(dve.tensor_scalar(
                        dt[b % 2][:, m, :], wide[:, pair, j * L:(j + 1) * L], b_dt[:, m:m + 1], 0.0, ALU.add, ALU.max))
                wait(act, ev["relu", b], got("xs", b))
                for j in range(2):
                    m = 2 * pair + j
                    ev["abs", b] = S["act"].after(act.activation(
                        conv[:, m, :], wide[:, pair, j * L:(j + 1) * L], ACT.Abs, bias=b_dt[:, m:m + 1]))

        def softplus_exp(b):
            wait(act, got("abs", b))
            ev["e", b] = S["act"].after(act.activation(conv[:], conv[:], ACT.Exp, scale=-1.0))

        def softplus_min(b):
            wait(dve, got("e", b), got("dt", b - 1))
            ev["f", b] = S["dve"].after(dve.tensor_scalar(soft[:], conv[:], LOG1P_SMALL, None, ALU.min))

        def softplus_series(b):
            wait(act, got("f", b), got("o_ps", b - 2))
            ev["series", b] = S["act"].after(act.activation(
                yT[b % 2][:], soft[:], ACT.Square, scale=3.0 ** -0.5, bias=series_bias[:]))
            ev["ln1p_e", b] = S["act"].after(act.activation(conv[:], conv[:], ACT.Ln, bias=1.0))
            wait(dve, ev["series", b])
            ev["log1p_f", b] = S["dve"].after(dve.scalar_tensor_tensor(
                out=yT[b % 2][:], in0=yT[b % 2][:], scalar=13.0 / 16.0, in1=soft[:], op0=ALU.add, op1=ALU.mult))

        def softplus_difference(b):
            wait(act, got("log1p_f", b))
            ev["ln1p_f", b] = S["act"].after(act.activation(soft[:], soft[:], ACT.Ln, bias=1.0))
            wait(dve, got("log1p_f", b), got("relu", b))
            ev["part", b] = S["dve"].after(dve.tensor_tensor(dt[b % 2][:], dt[b % 2][:], yT[b % 2][:], ALU.add))
            wait(pool, ev["ln1p_e", b], ev["ln1p_f", b])
            ev["bracket", b] = S["pool"].after(pool.tensor_tensor(conv[:], conv[:], soft[:], ALU.subtract))

        def softplus_sum(b):
            wait(dve, got("bracket", b), got("part", b))
            ev["dt", b] = S["dve"].after(dve.tensor_tensor(dt[b % 2][:], dt[b % 2][:], conv[:], ALU.add))

        def skip(b):
            wait(dve, got("xs", b), got("o_ps", b - 2))
            for m in range(M):
                ev["skip", b] = S["dve"].after(dve.tensor_scalar(
                    yT[b % 2][:, m, :], xs[b % 2][:, m, :], d_skip[:, m:m + 1], None, ALU.mult))
            wait(pool, ev["skip", b], got("dt", b), got("xd_ps", b))
            ev["u", b] = S["pool"].after(pool.tensor_tensor(xs[b % 2][:], xs[b % 2][:], dt[b % 2][:], ALU.mult))

        def chunk(b, c):
            q, pair = c // PAIRS, c % PAIRS
            g = b * SLOTS + c
            da, h = dA[g % 2], hs[g % 3]
            wait(act, got("dt", b), got("scan", g - 2))
            for j in range(2):
                m = 2 * pair + j
                for n in range(Q):
                    ev["dA", g] = ev["dA_all", b] = S["dA"].after(act.activation(
                        da[:, j, n, 1:L], dt[b % 2][:, m, 1:L], ACT.Exp, scale=a_neg[:, m, q * Q + n:q * Q + n + 1]))
            spread = lambda mat: mat[:].unsqueeze(1).broadcast_to([P, 2, Q, L])
            wait(pool, got("u", b), got("bc", b, q), got("y_ps", g - 3))
            ev["dbx", g] = S["dbx"].after(pool.tensor_tensor(
                h[:], xs[b % 2][:, 2 * pair:2 * pair + 2, :].unsqueeze(2).broadcast_to([P, 2, Q, L]),
                spread(bmat[q % 2]), ALU.mult))
            flat = h[:].rearrange("p j n l -> p (j n l)")
            wait(dve, ev["dA", g], ev["dbx", g])
            ev["scan", g] = S["scan"].after(dve.tensor_tensor_scan(
                flat, da[:].rearrange("p j n l -> p (j n l)"), flat, 0.0, ALU.mult, ALU.add))
            wait(dve, ev["scan", g], got("bc", b, q))
            ev["hc", g] = S["hc"].after(dve.tensor_tensor(h[:], h[:], spread(cmat[q % 2]), ALU.mult))

        def sum_states(g):
            wait(pe, got("hc", g), got("y", g - 2))
            for j in range(2):
                for n in range(Q):
                    mm = pe.matmul(yps[:, g % 2, j * L:(j + 1) * L], ident[:], hs[g % 3][:, j, n, :],
                                   start=(n == 0), stop=(n == Q - 1))
            ev["y_ps", g] = S["y_ps"].after(mm)

        def add_y(b, c):
            pair, g = c % PAIRS, b * SLOTS + c
            dst = yT[b % 2][:, 2 * pair:2 * pair + 2, :]
            wait(dve, got("y_ps", g), got("skip", b), got("y", g - PAIRS) if c >= PAIRS else None)
            ev["y", g] = S["evac"].after(dve.tensor_tensor(
                dst, dst, yps[:, g % 2, 0:2 * L].rearrange("p (j l) -> p j l", j=2), ALU.add))

        def gate(b):
            wait(pool, got("y", b * SLOTS + SLOTS - 1), got("zs", b))
            ev["gated", b] = S["pool"].after(pool.tensor_tensor(yT[b % 2][:], yT[b % 2][:], zs[b % 2][:], ALU.mult))

        def out_proj(b):
            wait(pe, got("gated", b), got("hT", min(b + 2, B - 1)))
            for i in range(2):
                for m in range(M):
                    mm = pe.matmul(narrow[0:TT, i, :], yT[b % 2][:, m, i * TT:(i + 1) * TT], w_out[:, m, :],
                                   start=(m == 0), stop=(m == M - 1))
                ev["o_ps", b] = ev["o_ps", b, i] = S["o_ps"].after(mm)

        def add_residual(b):
            for i in range(2):
                wait(dve, got("o_ps", b, i), got("res", b), got("rms", b))
                e = S["dve"].after(dve.tensor_tensor(xt[b % 3][:, i, :], xt[b % 3][:, i, :], narrow[0:TT, i, :], ALU.add))
            ev["x1", b] = e
            wait(sp, e)
            ev["x1_stored", b] = S[f"xout{b % 3}"].after(
                sp.dma_start(x1_dram[b].rearrange("(i p) d -> p i d", p=TT), xt[b % 3][:]), 16)
            wait(dve, e)
            for i in range(2):
                e = S["dve"].after(dve.bn_stats(stats1[:, i, :], xt[b % 3][:, i, :]))
            wait(dve, e)
            for i in range(2):
                e = S["dve"].after(dve.bn_aggr(mv1[:, 2 * b + i, :], stats1[:, i, :]))
            wait(dve, e)

        pieces = [w[r * P:(r + 1) * P, c * D:(c + 1) * D] for w in (t["w1"], t["w2"])
                  for r in range(w.shape[0] // P) for c in range(w.shape[1] // D)]
        assert len(pieces) <= B * SLOTS

        def load_piece(n):
            wait(sp, got("wsum", n - 2))
            ev["piece", n] = S[f"piece{n % 2}"].after(sp.dma_start(piece[n % 2][:], pieces[n]), 16)

        def sum_piece(n):
            wait(act, got("piece", n))
            ev["wsum", n] = S["act"].after(act.activation(
                piece[n % 2][:], piece[n % 2][:], ACT.Abs, accum_out=wsum[:, n:n + 1]))

        steps = [
            (-25, load_x), (-23, row_stats), (-22, lambda b: guess_rsqrt(b, "var", var_eps[:], 1.0)),
            (-21, normalise), (-20, mean_square), (-19, mean_square_eps),
            (-19, lambda b: guess_rsqrt(b, "ms", var_eps[:], 1.0)), (-18, rms), (-18, transpose_h), (-17, scale_hT),
            (-16, lambda b: project(b, 0, (0, 1), (got("zs", b - 1), got("relu", b - 1), got("abs", b - 1)), "x_ps")),
            (-15, lambda b: project(b, 0, (2, 3), (), "x_ps")),
            (-15, lambda b: (last_tap(b, 0), last_tap(b, 1))), (-14, lambda b: (last_tap(b, 2), last_tap(b, 3))),
            (-14, lambda b: (older_taps(b, 0), older_taps(b, 1))), (-13, lambda b: (older_taps(b, 2), older_taps(b, 3))),
            (-13, lambda b: project(b, M, (0, 1), (got("conv", b, 0), got("conv", b, 1)), "z_ps")),
            (-12, lambda b: project(b, M, (2, 3), (got("conv", b, 2), got("conv", b, 3)), "z_ps")),
            (-11, silus), (-10, x_dbl), (-9, keep_xd), (1 - PAIRS, lambda b: spread_bc(b, 0)), (-8, dt_raw),
            (-7, softplus_abs), (-6, softplus_exp), (-5, softplus_min), (-4, softplus_series),
            (-3, softplus_difference), (-2, softplus_sum), (-1, skip),
            *((q * PAIRS - PAIRS + 1, lambda b, q=q: spread_bc(b, q)) for q in range(1, 4)),
            (SLOTS + 1, gate), (SLOTS + 2, out_proj), (SLOTS + 3, add_residual),
        ]
        for slot in range(-25, B * SLOTS + 4):
            for b in range(B):
                at = slot - b * SLOTS
                if 1 <= at <= SLOTS:
                    sum_states(b * SLOTS + at - 1)
                if 0 <= at < SLOTS:
                    chunk(b, at)
                if 1 <= at <= SLOTS:
                    add_y(b, at - 1)
            for b in range(B):
                for offset, step in steps:
                    if slot - b * SLOTS == offset:
                        step(b)
            if slot >= 0:
                every = B * SLOTS // len(pieces)
                n = slot // every
                if n < len(pieces) and slot % every == 0:
                    load_piece(n)
                if n < len(pieces) and slot % every == every - 1:
                    sum_piece(n)
        for b in range(B - 3, B):
            wait(sp, ev["x1_stored", b])
        nc.all_engine_barrier()




def rstd_of_rows(nc, mem, mv, rstd, done_act, done_dve):
    rows, tiles, _ = mv.shape
    var_eps, guess, tmp = (mem.sbuf(n, [rows, tiles]) for n in ("row_var", "row_guess", "row_tmp"))
    e = done_dve.after(nc.vector.tensor_scalar(var_eps[:], mv[:, :, 1], EPS, None, ALU.add))
    wait(nc.scalar, e)
    wait(nc.scalar, done_act.after(nc.scalar.activation(guess[:], var_eps[:], ACT.Ln)))
    e = done_act.after(nc.scalar.activation(guess[:], guess[:], ACT.Exp, scale=-0.5))
    wait(nc.vector, e)
    return newton_rsqrt(nc.vector, done_dve, rstd[:], guess[:], var_eps[:], tmp[:])


def attention_phase(nc, t, x1_dram, x2_dram, mv1, mv2):
    B, D, KEYS = t["ctxT"].shape
    L = x1_dram.shape[1]
    TT = L // 2
    KD = D // P
    HEADS = 16
    DH = D // HEADS
    GROUP = P // DH
    GROUPS = HEADS // GROUP
    SLOTS = HEADS
    KC = 125
    CHUNKS = KEYS // KC
    HALF = KEYS // 2
    HPAD = HALF + HALF % 2
    KPAD = 2 * HPAD
    RING = GROUP + 1
    SCALE = float(DH) ** -0.5
    assert KC * CHUNKS == KEYS and CHUNKS % 2 == 0 and 2 * L <= BANK and HPAD <= BANK

    pe, act, dve, pool, sp = nc.tensor, nc.scalar, nc.vector, nc.gpsimd, nc.sync
    with ExitStack() as stack:
        mem = Memory(nc, stack, "b_")
        wk = [mem.sbuf(f"wk_{n}", [P, KD, D], F32R) for n in ("hi", "lo")]
        wv = [mem.sbuf(f"wv_{n}", [P, KD, D], F32R) for n in ("hi", "lo")]
        wq = mem.sbuf("wq", [P, KD, D])
        wo = mem.sbuf("wo", [P, KD, D])
        bq = mem.sbuf("bq", [P, KD])
        bk = mem.sbuf("bk", [P, KD])
        bv = mem.sbuf("bv", [P, D])
        bo = mem.sbuf("bo", [P, D])
        ident = mem.sbuf("ident", [P, P])
        mask = mem.sbuf("mask", [TT, 2, KEYS])
        rstd = mem.sbuf("rstd", [TT, 2 * B])
        raw = [mem.sbuf(f"raw{i}", [P, KPAD]) for i in range(2)]
        ctx = [mem.sbuf(f"ctx_{n}", [P, KD, KPAD], F32R) for n in ("hi", "lo")]
        k32 = mem.sbuf("k32", [P, HPAD])
        kT = [[mem.sbuf(f"kT{i}_{n}", [P, KPAD], F32R) for n in ("hi", "lo")] for i in range(2)]
        v = [mem.sbuf(f"v{i}", [KC, CHUNKS, D]) for i in range(2)]
        xt = [mem.sbuf(f"xt{i}", [TT, 2, D]) for i in range(2)]
        ln = mem.sbuf("ln", [TT, 2, D])
        stats = mem.sbuf("stats", [TT, 2, 6])
        hT = mem.sbuf("hT", [P, KD, L])
        q32 = mem.sbuf("q32", [P, L])
        qz = [[mem.sbuf(f"qz{i}_{n}", [P, GROUP, L], F32R) for n in ("hi", "lo")] for i in range(2)]
        sc = [mem.sbuf(f"sc{i}", [TT, 2, KEYS]) for i in range(2)]
        nmax = mem.sbuf("nmax", [TT, 2, HEADS])
        esum = mem.sbuf("esum", [TT, 2, HEADS])
        rsum = mem.sbuf("rsum", [TT, 2, GROUP])
        rwide = mem.sbuf("rwide", [TT, 2, GROUP, DH])
        pT = [mem.sbuf(f"pT{i}", [KC, CHUNKS, L]) for i in range(RING)]
        rb = mem.sbuf("rb", [P, L])
        oT = mem.sbuf("oT", [P, GROUPS, L])
        sps = mem.psum("sps", [P, 4, BANK])
        tps = mem.psum("tps", [P, 2, BANK])
        vps = mem.psum("vps", [P, BANK])
        ups = mem.psum("ups", [P, BANK])

        S = {n: mem.semaphore(n) for n in (
            "w", "raw0", "raw1", "xin0", "xin1", "xout0", "xout1", "const", "act", "dve", "pool",
            "unit", "s_ps", "ttr", "exp", "t_ps", "pt_act", "pt_dve", "pv", "ctx_hi", "ctx_lo", "k_hi", "k_lo",
            "q_hi", "q_lo", "free_act", "free_dve")}
        ev = {}

        def got(*key):
            assert key in ev or min(key[1:]) < 0, key
            return ev.get(key)

        for dst, src in (
            (wq[:], t["Wq"].rearrange("(k p) n -> p k n", p=P)), (wo[:], t["Wo"].rearrange("(k p) n -> p k n", p=P)),
            (bq[:], t["bq"]), (bk[:], t["bk"]), (ident[:], t["ident"]),
            (bv[:], t["bv"].partition_broadcast(P)), (bo[:], t["bo"].partition_broadcast(P)),
            (mask[:], t["mask"].rearrange("(i p) k -> p i k", p=TT)),
        ):
            weights = S["w"].after(act.dma_start(dst, src), 16)
        wait(dve, weights)
        S["const"].after(dve.tensor_scalar(bq[:], bq[:], SCALE, None, ALU.mult))
        S["const"].after(dve.tensor_scalar(mask[:], mask[:], NEG_INF_SCALE, None, ALU.mult))
        for i in range(2):
            for part in qz[i]:
                S["const"].after(dve.memset(part[:].bitcast(F32), 0.0))
            consts = S["const"].after(dve.memset(raw[i][:], 0.0))
        for engine in (pe, act, dve, pool, sp):
            wait(engine, weights, consts)
        rstd_ready = rstd_of_rows(nc, mem, mv1, rstd, S["act"], S["dve"])
        n = 0
        for w, name in ((wk, "Wk"), (wv, "Wv")):
            src = t[name].rearrange("(k p) n -> p k n", p=P)
            for k in range(KD):
                stage = raw[n % 2]
                wait(sp, got("raw_used", n - 2))
                e = S[f"raw{n % 2}"].after(sp.dma_start(stage[:, 0:D], src[:, k, :]), 16)
                wait(dve, e)
                e = S["ctx_hi"].after(dve.tensor_copy(w[0][:, k, :], stage[:, 0:D]))
                wait(pool, e)
                ev["raw_used", n] = S["ctx_lo"].after(
                    pool.tensor_tensor(w[1][:, k, :], stage[:, 0:D], w[0][:, k, :].bitcast(F32), ALU.subtract))
                n += 1
        split_weights = ev["raw_used", n - 1]
        wait(pe, split_weights)
        wait(dve, split_weights)
        for i in range(2):
            consts = S["const"].after(dve.memset(raw[i][:], 0.0))
        wait(sp, consts)
        TERMS = ((0, 0), (0, 1), (1, 0))

        def load_x1(b):
            wait(sp, got("x2_stored", b - 2))
            ev["x1", b] = S[f"xin{b % 2}"].after(
                sp.dma_start(xt[b % 2][:], x1_dram[b].rearrange("(i p) d -> p i d", p=TT)), 16)

        def normalise(b):
            wait(dve, got("x1", b), got("hT_ps", b - 1, 1), rstd_ready)
            for i in range(2):
                ev["ln", b] = S["dve"].after(dve.tensor_scalar(
                    ln[:, i, :], xt[b % 2][:, i, :], mv1[:, 2 * b + i, 0:1], rstd[:, 2 * b + i:2 * b + i + 1],
                    ALU.subtract, ALU.mult))
            wait(pool, ev["ln", b])
            for i in range(2):
                ev["res", b] = S["pool"].after(pool.tensor_tensor(xt[b % 2][:, i, :], xt[b % 2][:, i, :], bo[0:TT, :], ALU.add))

        last_free = [None]

        def unit_begins():
            wait(pe, last_free[0])

        def transpose_h(b, part):
            unit_begins()
            wait(pe, got("ln", b))
            for k2 in range(2):
                for i in range(2):
                    mm = pe.transpose(ups[:, k2 * L + i * TT:k2 * L + (i + 1) * TT],
                                      ln[:, i, (2 * part + k2) * P:(2 * part + k2 + 1) * P], ident[0:TT, 0:TT])
            ev["hT_ps", b, part] = S["unit"].after(mm)
            wait(act, ev["hT_ps", b, part], got("q_ps", b - 1, GROUPS - 1))
            ev["hT", b] = last_free[0] = S["free_act"].after(act.activation(
                hT[:, 2 * part:2 * part + 2, :], ups[:, 0:2 * L].rearrange("p (k l) -> p k l", k=2), ACT.Copy))

        def load_ctx(b):
            for k in range(KD):
                n = b * KD + k
                wait(sp, got("ctx_lo", n - 2))
                ev["raw", n] = S[f"raw{n % 2}"].after(
                    sp.dma_start(raw[n % 2][:, 0:KEYS], t["ctxT"][b].rearrange("(k p) s -> p k s", p=P)[:, k, :]), 16)
                wait(dve, ev["raw", n], got("k_ps", b - 1, GROUPS - 1, 1))
                ev["ctx_hi", n] = S["ctx_hi"].after(dve.tensor_copy(ctx[0][:, k, :], raw[n % 2][:]))
                wait(pool, ev["ctx_hi", n], got("k_ps", b - 1, GROUPS - 1, 1))
                ev["ctx_lo", n] = ev["ctx", b] = S["ctx_lo"].after(pool.tensor_tensor(
                    ctx[1][:, k, :], raw[n % 2][:], ctx[0][:, k, :].bitcast(F32), ALU.subtract))

        def project_k(b, g, half):
            G = b * GROUPS + g
            unit_begins()
            wait(pe, got("ctx", b))
            cols = slice(half * HPAD, (half + 1) * HPAD)
            for n, (i, j) in enumerate(TERMS):
                for k in range(KD):
                    mm = pe.matmul(ups[:, 0:HPAD], wk[i][:, k, g * P:(g + 1) * P], ctx[j][:, k, cols],
                                   start=(n == 0 and k == 0), stop=(n == 2 and k == KD - 1))
            ev["k_ps", b, g, half] = S["unit"].after(mm)
            wait(act, ev["k_ps", b, g, half], got("k_lo", 2 * G + half - 1))
            e = last_free[0] = S["free_act"].after(act.activation(
                k32[:], ups[:, 0:HPAD], ACT.Identity, bias=bk[:, g:g + 1]))
            hi, lo = kT[G % 2]
            wait(dve, e, got("s_ps", 4 * (G - 1) - 1))
            e = S["k_hi"].after(dve.tensor_copy(hi[:, cols], k32[:]))
            wait(pool, e, got("s_ps", 4 * (G - 1) - 1))
            ev["k_lo", 2 * G + half] = S["k_lo"].after(
                pool.tensor_tensor(lo[:, cols], k32[:], hi[:, cols].bitcast(F32), ALU.subtract))

        def project_v(b, c):
            unit_begins()
            wait(pe, got("ctx", b))
            for n, (i, j) in enumerate(TERMS):
                for k in range(KD):
                    mm = pe.matmul(ups[0:KC, :], ctx[i][:, k, c * KC:(c + 1) * KC], wv[j][:, k, :],
                                   start=(n == 0 and k == 0), stop=(n == 2 and k == KD - 1))
            e = S["unit"].after(mm)
            wait(dve, e, got("pv", b - 2, GROUPS - 1))
            ev["v", b] = last_free[0] = S["free_dve"].after(
                dve.tensor_tensor(v[b % 2][:, c, :], ups[0:KC, :], bv[0:KC, :], ALU.add))

        def project_q(b, g):
            G = b * GROUPS + g
            unit_begins()
            wait(pe, got("hT", b))
            for k in range(KD):
                mm = pe.matmul(ups[:, 0:L], wq[:, k, g * P:(g + 1) * P], hT[:, k, :], start=(k == 0), stop=(k == KD - 1))
            ev["q_ps", b, g] = S["unit"].after(mm)
            wait(act, ev["q_ps", b, g], got("q_lo", G - 1))
            e = last_free[0] = S["free_act"].after(act.activation(
                q32[:], ups[:, 0:L], ACT.Identity, bias=bq[:, g:g + 1], scale=SCALE))
            hi, lo = qz[G % 2]
            wait(dve, e, got("s_ps", 4 * (G - 1) - 1))
            for j in range(GROUP):
                rows = slice(j * DH, (j + 1) * DH)
                e = S["q_hi"].after(dve.tensor_copy(hi[rows, j, :], q32[rows, :]))
            wait(dve, e)
            for j in range(GROUP):
                rows = slice(j * DH, (j + 1) * DH)
                ev["q_lo", G] = S["q_lo"].after(dve.tensor_tensor(
                    lo[rows, j, :], q32[rows, :], hi[rows, j, :].bitcast(F32), ALU.subtract))

        def scores(n):
            G, j = n // GROUP, n % GROUP
            wait(pe, got("k_lo", 2 * G + 1), got("q_lo", G))
            for i in range(2):
                wait(pe, got("ttr", n - 1, i))
                for half in range(2):
                    for m, (a, c) in enumerate(TERMS):
                        mm = pe.matmul(sps[0:TT, 2 * i + half, 0:HPAD], qz[G % 2][a][:, j, i * TT:(i + 1) * TT],
                                       kT[G % 2][c][:, half * HALF:half * HALF + HPAD], start=(m == 0), stop=(m == 2))
                ev["s_ps", n, i] = ev["s_ps", n] = S["s_ps"].after(mm)

        def softmax(n):
            h = n % HEADS
            for i in range(2):
                wait(dve, got("s_ps", n, i), got("t_ps", n - 2))
                ev["ttr", n, i] = S["ttr"].after(dve.tensor_tensor_reduce(
                    out=sc[n % 2][:, i, :].rearrange("p (a k) -> p a k", a=2), in0=sps[0:TT, 2 * i:2 * i + 2, 0:HALF],
                    in1=mask[:, i, :].rearrange("p (a k) -> p a k", a=2), scale=-1.0, scalar=3.0e38,
                    op0=ALU.add, op1=ALU.min, accum_out=nmax[:, i, h:h + 1]))
            for i in range(2):
                wait(act, ev["ttr", n, i], got("rsum", n // GROUP - GROUPS))
                ev["exp", n] = S["exp"].after(act.activation(
                    sc[n % 2][:, i, :], sc[n % 2][:, i, :], ACT.Exp, scale=-1.0, bias=nmax[:, i, h:h + 1],
                    accum_out=esum[:, i, h:h + 1]))

        def transpose_p(n):
            wait(pe, got("exp", n))
            for pair in range(CHUNKS // 2):
                bank = (n * (CHUNKS // 2) + pair) % 2
                wait(pe, got("t_free", n * (CHUNKS // 2) + pair - 2))
                for c2 in range(2):
                    c = 2 * pair + c2
                    for i in range(2):
                        mm = pe.transpose(tps[0:KC, bank, c2 * L + i * TT:c2 * L + (i + 1) * TT],
                                          sc[n % 2][:, i, c * KC:(c + 1) * KC], ident[0:TT, 0:TT])
                e = ev["t_ps", n] = S["t_ps"].after(mm)
                dst = pT[n % RING][:, 2 * pair:2 * pair + 2, :]
                src = tps[0:KC, bank, 0:2 * L].rearrange("p (c l) -> p c l", c=2)
                G = (n - RING) // GROUP
                freed = got("pv", G // GROUPS, G % GROUPS) if n >= RING else None
                if bank == 0:
                    wait(act, e, freed)
                    ev["t_free", n * (CHUNKS // 2) + pair] = ev["pT_act", n] = S["pt_act"].after(
                        act.activation(dst, src, ACT.Copy))
                else:
                    wait(dve, e, freed)
                    ev["t_free", n * (CHUNKS // 2) + pair] = ev["pT_dve", n] = S["pt_dve"].after(
                        dve.tensor_copy(dst, src))

        def weigh_v(b, g):
            G = b * GROUPS + g
            first = G * GROUP
            wait(dve, got("exp", first + GROUP - 1), got("r_ps", G - 1))
            e = S["dve"].after(dve.reciprocal(rsum[:], esum[:, :, g * GROUP:(g + 1) * GROUP]))
            ev["rsum", G] = e
            wait(dve, e)
            for i in range(2):
                e = S["dve"].after(dve.tensor_copy(rwide[:, i], rsum[:, i, :].unsqueeze(2).broadcast_to([TT, GROUP, DH])))
            wait(pe, got("pT_act", first + GROUP - 1), got("pT_dve", first + GROUP - 1), got("v", b), got("oT", G - 1))
            for c in range(CHUNKS):
                for j in range(GROUP):
                    n = first + j
                    mm = pe.matmul(vps[j * DH:(j + 1) * DH, 0:L], v[b % 2][:, c, (g * GROUP + j) * DH:(g * GROUP + j + 1) * DH],
                                   pT[n % RING][:, c, :], start=(c == 0), stop=(c == CHUNKS - 1))
            ev["pv", b, g] = S["pv"].after(mm)
            unit_begins()
            wait(pe, e)
            for i in range(2):
                mm = pe.matmul(ups[:, i * TT:(i + 1) * TT], rwide[:, i].rearrange("p j d -> p (j d)"),
                               ident[0:TT, 0:TT], start=True, stop=True)
            ev["r_ps", G] = S["unit"].after(mm)
            wait(act, ev["r_ps", G], got("oT", G - 1))
            ev["rb", G] = last_free[0] = S["free_act"].after(act.activation(rb[:], ups[:, 0:L], ACT.Copy))

        def scale_o(b, g):
            G = b * GROUPS + g
            wait(dve, got("pv", b, g), got("rb", G), got("o_ps", b - 1))
            ev["oT", G] = S["dve"].after(dve.tensor_tensor(oT[:, g, :], vps[:, 0:L], rb[:], ALU.mult))

        def out_proj(b, i):
            unit_begins()
            wait(pe, got("oT", b * GROUPS + GROUPS - 1))
            for g in range(GROUPS):
                mm = pe.matmul(ups[0:TT, :], oT[:, g, i * TT:(i + 1) * TT], wo[:, g, :],
                               start=(g == 0), stop=(g == GROUPS - 1))
            ev["o_ps", b] = S["unit"].after(mm)
            wait(dve, ev["o_ps", b], got("res", b))
            e = last_free[0] = S["free_dve"].after(
                dve.tensor_tensor(xt[b % 2][:, i, :], xt[b % 2][:, i, :], ups[0:TT, :], ALU.add))
            wait(dve, e)
            e = S["dve"].after(dve.bn_stats(stats[:, i, :], xt[b % 2][:, i, :]))
            wait(dve, e)
            e = S["dve"].after(dve.bn_aggr(mv2[:, 2 * b + i, :], stats[:, i, :]))
            if i == 1:
                wait(sp, e)
                ev["x2_stored", b] = S[f"xout{b % 2}"].after(
                    sp.dma_start(x2_dram[b].rearrange("(i p) d -> p i d", p=TT), xt[b % 2][:]), 16)

        steps = [
            (-9, load_x1), (-7, normalise), (-6, load_ctx),
            (-5, lambda b: transpose_h(b, 0)), (-4, lambda b: transpose_h(b, 1)),
            *((4 * g - 4 + half, lambda b, g=g, half=half: project_k(b, g, half))
              for g in range(GROUPS) for half in range(2)),
            *((4 * g - 2, lambda b, g=g: project_q(b, g)) for g in range(GROUPS)),
            (-3, lambda b: project_v(b, 0)), (-2, lambda b: project_v(b, 1)), (-2, lambda b: project_v(b, 2)),
            (-1, lambda b: project_v(b, 3)), (-1, lambda b: project_v(b, 4)), (0, lambda b: project_v(b, 5)),
            *((4 * g + 5, lambda b, g=g: weigh_v(b, g)) for g in range(GROUPS)),
            *((4 * g + 6, lambda b, g=g: scale_o(b, g)) for g in range(GROUPS)),
            (SLOTS + 3, lambda b: out_proj(b, 0)), (SLOTS + 4, lambda b: out_proj(b, 1)),
        ]
        for slot in range(-9, B * SLOTS + 5):
            if 0 <= slot < B * SLOTS:
                scores(slot)
                softmax(slot)
            for b in range(B):
                for offset, step in steps:
                    if slot - b * SLOTS == offset:
                        step(b)
            if 1 <= slot <= B * SLOTS:
                transpose_p(slot - 1)
        for b in range(B - 2, B):
            wait(sp, ev["x2_stored", b])
        nc.all_engine_barrier()


def ffn_phase(nc, t, x2_dram, out, mv2, wsum):
    B, L, D = x2_dram.shape
    TT = L // 2
    TILES = 4
    T = TILES * TT
    STEPS = B * L // T
    KD = D // P
    F = t["w1"].shape[0]
    FT = F // P
    LAG = 2
    assert T <= BANK and D <= BANK and wsum.shape[1] == FT + F // D * KD

    pe, act, dve, pool, sp = nc.tensor, nc.scalar, nc.vector, nc.gpsimd, nc.sync
    with ExitStack() as stack:
        mem = Memory(nc, stack, "c_")
        s1 = mem.sbuf("s1", [P, KD, F], F32R)
        s2 = mem.sbuf("s2", [P, FT, D], F32R)
        raw = [mem.sbuf(f"raw{i}", [P, F]) for i in range(2)]
        b1 = mem.sbuf("b1", [P, FT])
        b2 = mem.sbuf("b2", [P, D])
        ident = mem.sbuf("ident", [P, P])
        ones = mem.sbuf("ones", [P, P])
        alpha1 = mem.sbuf("alpha1", [P, FT])
        alpha2 = mem.sbuf("alpha2", [P, KD])
        diag = mem.sbuf("diag", [P, KD, P])
        alpha2_row = mem.sbuf("alpha2_row", [P, D])
        rstd = mem.sbuf("rstd", [TT, 2 * B])
        xt = [mem.sbuf(f"xt{i}", [TT, TILES, D]) for i in range(3)]
        ln = mem.sbuf("ln", [TT, TILES, D])
        hT = [[mem.sbuf(f"hT{i}_{n}", [P, KD, T], F32R) for n in ("hi", "lo")] for i in range(2)]
        g32 = [mem.sbuf(f"g32_{i}", [P, T]) for i in range(2)]
        gT = [[mem.sbuf(f"gT{i}_{n}", [P, T], F32R) for n in ("hi", "lo")] for i in range(LAG + 1)]
        prod = [mem.sbuf(f"prod{i}", [TT, D]) for i in range(2)]
        tps = mem.psum("tps", [P, BANK])
        fps = mem.psum("fps", [P, 3, BANK])
        ops = mem.psum("ops", [P, TILES, BANK])

        S = {n: mem.semaphore(n) for n in (
            "w", "raw0", "raw1", "xin0", "xin1", "xin2", "xout0", "xout1", "xout2", "const", "act", "dve",
            "sign1", "sign2", "pool", "t_ps", "h_hi", "h_lo", "f_ps", "gelu", "g_hi", "g_lo", "o_ps", "prod", "sum")}
        ev = {}

        def got(*key):
            assert key in ev or min(key[1:]) < 0, key
            return ev.get(key)

        for dst, src in ((b1[:], t["b1"]), (ident[:], t["ident"]), (b2[:], t["b2"].partition_broadcast(P))):
            weights = S["w"].after(act.dma_start(dst, src), 16)
        rstd_ready = rstd_of_rows(nc, mem, mv2, rstd, S["act"], S["dve"])

        w1T = t["w1T"].rearrange("(k p) f -> p k f", p=P)
        w2T = t["w2T"].rearrange("(a c p) d -> a p c d", p=P, c=F // D)
        loads = [(w1T[:, k, :], s1[:, k, :], "sign1") for k in range(KD)]
        loads += [(w2T[a], s2[:, a * (F // D):(a + 1) * (F // D), :], "sign2") for a in range(KD)]
        for n, (src, dst, name) in enumerate(loads):
            stage = raw[n % 2][:] if name == "sign1" else raw[n % 2][:].rearrange("p (c d) -> p c d", d=D)
            wait(sp, got("sign", n - 2))
            e = S[f"raw{n % 2}"].after(sp.dma_start(stage, src), 16)
            wait(act, e)
            ev["sign", n] = S[name].after(act.activation(dst, stage, ACT.Sign))
        signs1, signs2 = ev["sign", KD - 1], ev["sign", 2 * KD - 1]

        for engine in (dve, pe, act, pool):
            wait(engine, weights)
        alpha1_ready = S["const"].after(dve.tensor_scalar(alpha1[:], wsum[:, 0:FT], 1.0 / D, None, ALU.mult))
        e = S["const"].after(dve.tensor_reduce(
            alpha2[:], wsum[:, FT:].rearrange("p (r c) -> p r c", c=F // D), AX_X, ALU.add))
        wait(dve, e)
        for k in range(KD):
            S["const"].after(dve.tensor_scalar(diag[:, k, :], ident[:], alpha2[:, k:k + 1], 1.0 / F, ALU.mult, ALU.mult))
        e = S["const"].after(dve.memset(ones[:], 1.0))
        wait(pe, e)
        for k in range(KD):
            mm = pe.matmul(tps[:, k * P:(k + 1) * P], ones[:], diag[:, k, :], start=True, stop=True)
        e = S["t_ps"].after(mm)
        wait(dve, e)
        alpha2_ready = S["const"].after(dve.tensor_copy(alpha2_row[:], tps[:, 0:D]))
        wait(pe, alpha2_ready)
        wait(act, alpha1_ready)

        x2_tiles = x2_dram.rearrange("b (i p) d -> p (b i) d", p=TT)
        out_tiles = out.rearrange("b (i p) d -> p (b i) d", p=TT)

        def load_x2(c):
            wait(sp, got("stored", c - 3))
            ev["x2", c] = S[f"xin{c % 3}"].after(
                sp.dma_start(xt[c % 3][:], x2_tiles[:, TILES * c:TILES * (c + 1), :]), 16)

        def normalise(c):
            wait(dve, got("x2", c), got("h_ps", c - 1, KD - 1), rstd_ready)
            for i in range(TILES):
                n = TILES * c + i
                ev["ln", c] = S["dve"].after(dve.tensor_scalar(
                    ln[:, i, :], xt[c % 3][:, i, :], mv2[:, n, 0:1], rstd[:, n:n + 1], ALU.subtract, ALU.mult))
            wait(pool, ev["ln", c])
            for i in range(TILES):
                ev["res", c] = S["pool"].after(pool.tensor_tensor(
                    xt[c % 3][:, i, :], xt[c % 3][:, i, :], b2[0:TT, :], ALU.add))

        def transpose_h(c, k):
            wait(pe, got("ln", c), got("h_lo", c, k - 1) if k else got("h_lo", c - 1, KD - 1))
            for i in range(TILES):
                mm = pe.transpose(tps[:, i * TT:(i + 1) * TT], ln[:, i, k * P:(k + 1) * P], ident[0:TT, 0:TT])
            ev["h_ps", c, k] = S["t_ps"].after(mm)
            hi, lo = hT[c % 2]
            used = got("f_ps", (c - 2) * FT + FT - 1)
            wait(act, ev["h_ps", c, k], used)
            e = S["h_hi"].after(act.activation(hi[:, k, :], tps[:, 0:T], ACT.Copy))
            wait(dve, e, used)
            ev["h_lo", c, k] = S["h_lo"].after(
                dve.tensor_tensor(lo[:, k, :], tps[:, 0:T], hi[:, k, :].bitcast(F32), ALU.subtract))

        def hidden(n):
            c, f = n // FT, n % FT
            wait(pe, got("h_lo", c, KD - 1), signs1, got("gelu", n - 3))
            for k in range(KD):
                for part in range(2):
                    mm = pe.matmul(fps[:, n % 3, 0:T], s1[:, k, f * P:(f + 1) * P], hT[c % 2][part][:, k, :],
                                   start=(k == 0 and part == 0), stop=(k == KD - 1 and part == 1))
            ev["f_ps", n] = S["f_ps"].after(mm)
            wait(act, ev["f_ps", n], got("g_lo", n - 2))
            ev["gelu", n] = S["gelu"].after(act.activation(
                g32[n % 2][:], fps[:, n % 3, 0:T], ACT.Gelu, scale=alpha1[:, f:f + 1], bias=b1[:, f:f + 1]))
            hi, lo = gT[n % (LAG + 1)]
            wait(dve, ev["gelu", n], got("o_ps", n - LAG - 1))
            e = S["g_hi"].after(dve.tensor_copy(hi[:], g32[n % 2][:]))
            wait(pool, e, got("o_ps", n - LAG - 1))
            ev["g_lo", n] = S["g_lo"].after(pool.tensor_tensor(lo[:], g32[n % 2][:], hi[:].bitcast(F32), ALU.subtract))

        def second(n):
            c, f = n // FT, n % FT
            wait(pe, got("g_lo", n), signs2)
            for i in range(TILES):
                if f == 0:
                    wait(pe, got("prod", c - 1, i))
                for part in range(2):
                    mm = pe.matmul(ops[0:TT, i, :], gT[n % (LAG + 1)][part][:, i * TT:(i + 1) * TT], s2[:, f, :],
                                   start=(f == 0 and part == 0), stop=(f == FT - 1 and part == 1))
                if f == FT - 1:
                    ev["o_tile", c, i] = S["o_ps"].after(mm)
            ev["o_ps", n] = S["o_ps"].after(mm) if f < FT - 1 else ev["o_tile", c, TILES - 1]

        def finish(c):
            for i in range(TILES):
                m = c * TILES + i
                wait(dve, ev["o_tile", c, i], got("sum", m - 2))
                ev["prod", c, i] = S["prod"].after(
                    dve.tensor_tensor(prod[m % 2][:], ops[0:TT, i, :], alpha2_row[0:TT, :], ALU.mult))
                wait(pool, ev["prod", c, i], got("res", c))
                ev["sum", m] = S["sum"].after(
                    pool.tensor_tensor(xt[c % 3][:, i, :], xt[c % 3][:, i, :], prod[m % 2][:], ALU.add))
            wait(sp, ev["sum", m])
            ev["stored", c] = S[f"xout{c % 3}"].after(
                sp.dma_start(out_tiles[:, TILES * c:TILES * (c + 1), :], xt[c % 3][:]), 16)

        steps = [(-12, load_x2), (-8, normalise), *((k - 6, lambda c, k=k: transpose_h(c, k)) for k in range(KD)),
                 (FT + LAG - 1, finish)]
        for slot in range(-12, STEPS * FT + LAG + 1):
            if 0 <= slot < STEPS * FT:
                hidden(slot)
            if LAG <= slot < STEPS * FT + LAG:
                second(slot - LAG)
            for c in range(STEPS):
                for offset, step in steps:
                    if slot - c * FT == offset:
                        step(c)
        for c in range(STEPS - 3, STEPS):
            wait(sp, ev["stored", c])


def decoder_layer(nc, t, out):
    B, L, D = t["x"].shape
    TT = L // 2
    N = t["A_log"].shape[1]
    F = t["w1"].shape[0]
    x1_dram = nc.dram_tensor("x1_scratch", (B, L, D), F32).ap()
    x2_dram = nc.dram_tensor("x2_scratch", (B, L, D), F32).ap()
    bc_dram = nc.dram_tensor("bc_scratch", (B, 2 * N, L), F32).ap()
    with ExitStack() as stack:
        mem = Memory(nc, stack, "")
        mv1 = mem.sbuf("mv1", [TT, 2 * B, 2])
        mv2 = mem.sbuf("mv2", [TT, 2 * B, 2])
        wsum = mem.sbuf("wsum", [P, F // P + F // D * (D // P)])
        mamba_phase(nc, t, x1_dram, bc_dram, mv1, wsum)
        attention_phase(nc, t, x1_dram, x2_dram, mv1, mv2)
        ffn_phase(nc, t, x2_dram, out, mv2, wsum)


def kernel(**inputs):
    import concourse.bacc as bacc
    from concourse.bass_utils import run_bass_kernel_spmd

    def columns(a):
        return np.asarray(a).reshape(-1, P).T

    i = {k: np.asarray(v) for k, v in inputs.items()}
    mamba = {k: i["L0_attn_" + k] for k in ("W_in", "conv_w", "W_x", "W_dt", "A_log", "W_out")}
    mamba |= {k: columns(i["L0_attn_" + k]) for k in ("norm_w", "conv_b", "b_dt", "D")}
    xattn = {k: i["L0_xattn_" + k] for k in ("Wq", "Wk", "Wv", "Wo", "bv", "bo")}
    xattn |= {k: columns(i["L0_xattn_" + k]) for k in ("bq", "bk")}
    ffn = {"w1": i["L0_ffn_w1"], "w2": i["L0_ffn_w2"], "w1T": i["L0_ffn_w1"].T, "w2T": i["L0_ffn_w2"].T,
           "b1": columns(i["L0_ffn_b1"]), "b2": i["L0_ffn_b2"]}
    arrays = {"x": i["x"], "ctxT": i["ctx_1024"].transpose(0, 2, 1), "mask": i["mask_1x1xSxS2_fk1"][0, 0],
              "ident": np.eye(P, dtype=np.float32), **mamba, **xattn, **ffn}
    arrays = {k: np.ascontiguousarray(a) for k, a in arrays.items()}

    nc = bacc.Bacc("TRN2", target_bir_lowering=False, num_devices=1)
    t = {k: nc.dram_tensor(k + "_dram", a.shape, mybir.dt.from_np(a.dtype), kind="ExternalInput").ap()
         for k, a in arrays.items()}
    out = nc.dram_tensor("out_dram", i["x"].shape, F32, kind="ExternalOutput").ap()
    decoder_layer(nc, t, out)
    result = run_bass_kernel_spmd(nc, [{k + "_dram": a for k, a in arrays.items()}], core_ids=[0])
    return result.results[0]["out_dram"]
```

```python
from contextlib import ExitStack

import numpy as np

import concourse.bass as bass
from concourse import mybir

P = 128
F32 = mybir.dt.float32
F32R = mybir.dt.float32r
ALU = mybir.AluOpType
ACT = mybir.ActivationFunctionType
AX_X = mybir.AxisListType.X
BANK = 512
EPS = 1e-5
NEG_INF_SCALE = -1e9
LOG1P_SMALL = 2.0 ** -8


class Counted:

    def __init__(self, sem):
        self.sem, self.value = sem, 0

    def after(self, instruction, by=1):
        instruction.then_inc(self.sem, by)
        self.value += by
        return self.sem, self.value


def wait(engine, *events):
    for event in events:
        if event is not None:
            engine.wait_ge(*event)


class Memory:

    def __init__(self, nc, stack, prefix):
        self.nc, self.stack, self.prefix = nc, stack, prefix

    def sbuf(self, name, shape, dtype=F32):
        return self.stack.enter_context(self.nc.sbuf_tensor(self.prefix + name, shape, dtype))

    def psum(self, name, shape):
        return self.stack.enter_context(self.nc.psum_tensor(self.prefix + name, shape, F32))

    def semaphore(self, name):
        return Counted(self.stack.enter_context(self.nc.semaphore(self.prefix + name)))


def newton_rsqrt(dve, done, out, guess, value, tmp):
    wait(dve, done.after(dve.tensor_tensor(tmp, guess, guess, ALU.mult)))
    wait(dve, done.after(dve.tensor_tensor(tmp, tmp, value, ALU.mult)))
    wait(dve, done.after(dve.tensor_scalar(tmp, tmp, -0.5, 1.5, ALU.mult, ALU.add)))
    event = done.after(dve.tensor_tensor(out, tmp, guess, ALU.mult))
    wait(dve, event)
    return event


def mamba_phase(nc, t, x1_dram, bc_dram, mv1, wsum):
    B, L, D = t["x"].shape
    TT = L // 2
    KD = D // P
    DI = t["W_out"].shape[0]
    M = DI // P
    R = t["W_dt"].shape[0]
    N = t["A_log"].shape[1]
    Q = N // 4
    TAPS = t["conv_w"].shape[1]
    DA = 2
    PAIRS = M // 2
    SLOTS = 4 * PAIRS
    assert TT <= P and 2 * L <= BANK and R + 2 * N <= P

    pe, act, dve, pool, sp = nc.tensor, nc.scalar, nc.vector, nc.gpsimd, nc.sync
    with ExitStack() as stack:
        mem = Memory(nc, stack, "a_")
        w_in = mem.sbuf("w_in", [P, KD, 2 * DI])
        w_out = mem.sbuf("w_out", [P, M, D])
        w_x = mem.sbuf("w_x", [P, M, R + 2 * N])
        w_dt = mem.sbuf("w_dt", [R, DI])
        a_neg = mem.sbuf("a_neg", [P, M, N])
        norm_w = mem.sbuf("norm_w", [P, KD])
        conv_w = mem.sbuf("conv_w", [P, M, TAPS])
        conv_b = mem.sbuf("conv_b", [P, M])
        b_dt = mem.sbuf("b_dt", [P, M])
        d_skip = mem.sbuf("d_skip", [P, M])
        ident = mem.sbuf("ident", [P, P])
        log_small = mem.sbuf("log_small", [P, 1])
        series_bias = mem.sbuf("series_bias", [P, 1])
        xt = [mem.sbuf(f"xt{i}", [TT, 2, D]) for i in range(3)]
        h = mem.sbuf("h", [TT, 2, D])
        stats = mem.sbuf("stats", [TT, 2, 6])
        mv = mem.sbuf("mv", [TT, 2, 2])
        squares = mem.sbuf("squares", [TT, 2, 2])
        guess = mem.sbuf("guess", [TT, 2, 2])
        ntmp = mem.sbuf("ntmp", [TT, 2, 2])
        rsqrt = mem.sbuf("rsqrt", [TT, 2, 2])
        gain = mem.sbuf("gain", [TT, 2, 2])
        stats1 = mem.sbuf("stats1", [TT, 2, 6])
        hT = mem.sbuf("hT", [P, KD, L])
        conv = mem.sbuf("conv", [P, M, L])
        xs = [mem.sbuf(f"xs{i}", [P, M, L]) for i in range(2)]
        zs = [mem.sbuf(f"zs{i}", [P, M, L]) for i in range(2)]
        dt = [mem.sbuf(f"dt{i}", [P, M, L]) for i in range(2)]
        yT = [mem.sbuf(f"yT{i}", [P, M, L]) for i in range(2)]
        piece = [mem.sbuf(f"piece{i}", [P, D]) for i in range(2)]
        xd = mem.sbuf("xd", [R + 2 * N, L])
        bmat = [mem.sbuf(f"bmat{i}", [P, Q, L]) for i in range(4)]
        cmat = [mem.sbuf(f"cmat{i}", [P, Q, L]) for i in range(4)]
        dA = [mem.sbuf(f"dA{i}", [P, 2, Q, L]) for i in range(DA)]
        hs = [mem.sbuf(f"hs{i}", [P, 2, Q, L]) for i in range(3)]
        work = mem.psum("work", [P, 6, BANK])
        yps = mem.psum("yps", [P, 2, BANK])

        S = {n: mem.semaphore(n) for n in (
            "w", "xin0", "xin1", "xin2", "xout0", "xout1", "xout2", "piece0", "piece1", "bcst", "bc0", "bc1", "bc2", "bc3",
            "const", "dve", "act", "pool", "work", "y_ps",
            "dA", "dbx", "u", "scan", "hc", "evac", "xs_done", "zs_done")}

        k_in = t["W_in"].rearrange("(k p) m -> p k m", p=P)
        for k in range(KD):
            S["w"].after(sp.dma_start(w_in[:, k, :], k_in[:, k, :]), 16)
        for dst, src in (
            (w_out[:], t["W_out"].rearrange("(m p) d -> p m d", p=P)),
            (w_x[:], t["W_x"].rearrange("(m p) r -> p m r", p=P)),
            (w_dt[:], t["W_dt"]),
            (a_neg[:], t["A_log"].rearrange("(m p) n -> p m n", p=P)),
            (norm_w[:], t["norm_w"]), (conv_w[:], t["conv_w"].rearrange("(m p) k -> p m k", p=P)),
            (conv_b[:], t["conv_b"]), (b_dt[:], t["b_dt"]), (d_skip[:], t["D"]), (ident[:], t["ident"]),
        ):
            weights = S["w"].after(act.dma_start(dst, src), 16)
        act.preload_act_table_set("natural_log_exp_and_others")
        wait(act, weights)
        e = S["act"].after(act.activation(a_neg[:], a_neg[:], ACT.Exp))
        wait(dve, e)
        S["const"].after(dve.tensor_scalar(a_neg[:], a_neg[:], -1.0, None, ALU.mult))
        S["const"].after(dve.memset(series_bias[:], -(3.0 ** 0.5) / 4.0))
        e = S["const"].after(dve.memset(log_small[:], LOG1P_SMALL))
        wait(act, e)
        e = S["act"].after(act.activation(log_small[:], log_small[:], ACT.Ln, bias=1.0))
        wait(dve, e)
        for i in range(DA):
            consts = S["const"].after(dve.memset(dA[i][:, :, :, 0:1], 0.0))
        for engine in (pe, act, dve, pool):
            wait(engine, weights, consts)

        ev = {}

        def got(*key):
            assert key in ev or min(key[1:]) < 0, key
            return ev.get(key)

        def load_x(b):
            wait(sp, got("x1_stored", b - 3))
            ev["x", b] = S[f"xin{b % 3}"].after(
                sp.dma_start(xt[b % 3][:], t["x"][b].rearrange("(i p) d -> p i d", p=TT)), 16)

        def row_stats(b):
            wait(dve, got("x", b))
            for i in range(2):
                e = S["dve"].after(dve.bn_stats(stats[:, i, :], xt[b % 3][:, i, :]))
            wait(dve, e)
            for i in range(2):
                e = S["dve"].after(dve.bn_aggr(mv[:, i, :], stats[:, i, :]))
            wait(dve, e)
            e = S["dve"].after(dve.tensor_scalar(squares[:, 0, :], mv[:, :, 1], EPS, None, ALU.add))
            wait(dve, e)
            e = S["dve"].after(dve.reciprocal(ntmp[:, 0, :], squares[:, 0, :]))
            wait(dve, e)
            e = S["dve"].after(dve.tensor_tensor(ntmp[:, 1, :], ntmp[:, 0, :], mv[:, :, 1], ALU.mult))
            wait(dve, e)
            ev["squares", b] = S["dve"].after(dve.tensor_scalar(squares[:, 1, :], ntmp[:, 1, :], EPS, None, ALU.add))

        def guess_rsqrt(b):
            wait(act, got("squares", b))
            e = S["act"].after(act.activation(guess[:], squares[:], ACT.Ln))
            wait(act, e)
            ev["guess", b] = S["act"].after(act.activation(guess[:], guess[:], ACT.Exp, scale=-0.5))

        def normalise(b):
            wait(dve, got("guess", b))
            newton_rsqrt(dve, S["dve"], rsqrt[:], guess[:], squares[:], ntmp[:])
            S["dve"].after(dve.tensor_tensor(ntmp[:, 0, :], rsqrt[:, 0, :], rsqrt[:, 1, :], ALU.mult))
            S["dve"].after(dve.tensor_scalar(gain[:, 0, :], rsqrt[:, 0, :], 1.0, None, ALU.add))
            e = S["dve"].after(dve.tensor_tensor(gain[:, 1, :], rsqrt[:, 0, :], mv[:, :, 0], ALU.mult))
            wait(dve, e, got("hT_read", b - 1))
            for i in range(2):
                e = ev["h", b] = S["dve"].after(dve.tensor_scalar(
                    h[:, i, :], xt[b % 3][:, i, :], mv[:, i, 0:1], ntmp[:, 0, i:i + 1], ALU.subtract, ALU.mult))
            wait(dve, e)
            for i in range(2):
                ev["res", b] = S["dve"].after(dve.tensor_scalar(
                    xt[b % 3][:, i, :], xt[b % 3][:, i, :], gain[:, 0, i:i + 1], gain[:, 1, i:i + 1],
                    ALU.mult, ALU.subtract))

        freed = [None] * 6
        turn = [0]

        def next_bank():
            bank = turn[0] % 6
            turn[0] += 1
            wait(pe, freed[bank])
            return bank

        def transpose_h(b):
            wait(pe, got("h", b))
            for half in range(2):
                bank = ev["hT_bank", b, half] = next_bank()
                for k in range(2 * half, 2 * half + 2):
                    for i in range(2):
                        col = (k % 2) * L + i * TT
                        mm = pe.transpose(work[:, bank, col:col + TT], h[:, i, k * P:(k + 1) * P], ident[0:TT, 0:TT])
                ev["hT_ps", b, half] = ev["hT_read", b] = S["work"].after(mm)

        def scale_hT(b):
            for k in range(KD):
                bank = ev["hT_bank", b, k // 2]
                wait(dve, got("hT_ps", b, k // 2), got("part", b - 1, 1))
                ev["hT", b] = freed[bank] = S["dve"].after(dve.tensor_scalar(
                    hT[:, k, :], work[:, bank, (k % 2) * L:(k % 2 + 1) * L], norm_w[:, k:k + 1], None, ALU.mult))

        def project(b, name, pair):
            first = 2 * pair + (M if name == "z_ps" else 0)
            wait(pe, got("hT", b))
            bank = ev[name + "_bank", b, pair] = next_bank()
            for j in range(2):
                for k in range(KD):
                    mm = pe.matmul(work[:, bank, j * L:(j + 1) * L], w_in[:, k, (first + j) * P:(first + j + 1) * P],
                                   hT[:, k, :], start=(k == 0), stop=(k == KD - 1))
            ev[name, b, pair] = S["work"].after(mm)

        def keep_z(b, pair):
            bank = ev["z_ps_bank", b, pair]
            wait(act, got("z_ps", b, pair), got("gated", b - 2))
            ev["z", b] = freed[bank] = S["act"].after(act.activation(
                zs[b % 2][:, 2 * pair:2 * pair + 2, :],
                work[:, bank, 0:2 * L].rearrange("p (j l) -> p j l", j=2), ACT.Copy))

        def last_tap(b, pair):
            bank = ev["x_ps_bank", b, pair]
            wait(act, got("x_ps", b, pair), got("dt", b - 1))
            for j in range(2):
                m = 2 * pair + j
                e = S["act"].after(act.activation(conv[:, m, :], work[:, bank, j * L:(j + 1) * L], ACT.Identity,
                                                  scale=conv_w[:, m, TAPS - 1:TAPS], bias=conv_b[:, m:m + 1]))
            ev["tap", b, pair] = e

        def older_taps(b, pair):
            bank = ev["x_ps_bank", b, pair]
            wait(dve, got("tap", b, pair))
            for back in range(1, TAPS):
                for j in range(2):
                    m = 2 * pair + j
                    e = S["dve"].after(dve.scalar_tensor_tensor(
                        out=conv[:, m, back:], in0=work[:, bank, j * L:(j + 1) * L - back],
                        scalar=conv_w[:, m, TAPS - 1 - back:TAPS - back], in1=conv[:, m, back:],
                        op0=ALU.mult, op1=ALU.add))
                wait(dve, e)
            ev["conv", b, pair] = freed[bank] = e

        def silus(b):
            wait(act, *(got("conv", b, p) for p in range(PAIRS)), got("z", b), got("dbx_all", b - 2))
            ev["xs", b] = S["xs_done"].after(act.activation(xs[b % 2][:], conv[:], ACT.Silu))
            ev["zs", b] = S["zs_done"].after(act.activation(zs[b % 2][:], zs[b % 2][:], ACT.Silu))
            act.preload_act_table_set("natural_log_exp_and_others")

        def x_dbl(b):
            wait(pe, got("xs", b))
            bank = ev["xd_bank", b] = next_bank()
            for m in range(M):
                mm = pe.matmul(work[0:R + 2 * N, bank, 0:L], w_x[:, m, :], xs[b % 2][:, m, :],
                               start=(m == 0), stop=(m == M - 1))
            ev["xd_ps", b] = S["work"].after(mm)

        def keep_xd(b):
            bank = ev["xd_bank", b]
            wait(dve, got("xd_ps", b), got("dt_ps", b - 1, PAIRS - 1), got("bc_stored", b - 1))
            ev["xd", b] = freed[bank] = S["dve"].after(dve.tensor_copy(xd[:], work[0:R + 2 * N, bank, 0:L]))
            wait(sp, ev["xd", b])
            ev["bc_stored", b] = S["bcst"].after(sp.dma_start(bc_dram[b], xd[R:R + 2 * N, :]), 16)

        def spread_bc(b, q):
            wait(sp, got("bc_stored", b), got("hc", b * SLOTS + q - 4))
            for dst, row in ((bmat[q], q * Q), (cmat[q], N + q * Q)):
                src = bc_dram[b, row:row + Q, :].partition_broadcast(P)
                ev["bc", b, q] = S[f"bc{q}"].after(sp.dma_start(dst[:], src), 16)

        def dt_raw(b):
            wait(pe, got("xd", b))
            for pair in range(PAIRS):
                bank = ev["dt_bank", b, pair] = next_bank()
                for j in range(2):
                    m = 2 * pair + j
                    mm = pe.matmul(work[:, bank, j * L:(j + 1) * L], w_dt[:, m * P:(m + 1) * P], xd[0:R, :],
                                   start=True, stop=True)
                ev["dt_ps", b, pair] = S["work"].after(mm)

        def softplus_tables(b):
            for pair in range(PAIRS):
                wait(act, got("dt_ps", b, pair), got("xs", b))
                bank = ev["dt_bank", b, pair]
                for j in range(2):
                    m = 2 * pair + j
                    e = ev["abs", b, pair] = S["act"].after(act.activation(
                        conv[:, m, :], work[:, bank, j * L:(j + 1) * L], ACT.Abs, bias=b_dt[:, m:m + 1]))
            wait(act, e)
            e = S["act"].after(act.activation(conv[:], conv[:], ACT.Exp, scale=-1.0))
            wait(act, e, got("z_ps", b, PAIRS - 1), got("o_ps", b - 2))
            ev["log", b] = S["act"].after(act.activation(yT[b % 2][:], conv[:], ACT.Ln, bias=1.0))
            square_half(b, 0)

        def square_half(b, half):
            wait(act, got("part", b, 0) if half else None)
            ev["square", b, half] = S["act"].after(act.activation(
                hT[:], conv[:, half * PAIRS:(half + 1) * PAIRS, :], ACT.Square, scale=3.0 ** -0.5, bias=series_bias[:]))

        def softplus_relu(b):
            for pair in range(PAIRS):
                bank = ev["dt_bank", b, pair]
                wait(dve, ev["abs", b, pair], got("dA_all", b - 2), got("u", b - 2))
                for j in range(2):
                    m = 2 * pair + j
                    ev["relu", b] = freed[bank] = S["dve"].after(dve.tensor_scalar(
                        dt[b % 2][:, m, :], work[:, bank, j * L:(j + 1) * L], b_dt[:, m:m + 1], 0.0, ALU.add, ALU.max))

        def softplus_series(b, half):
            tiles = slice(half * PAIRS, (half + 1) * PAIRS)
            wait(dve, ev["square", b, half])
            e = S["dve"].after(dve.scalar_tensor_tensor(
                out=hT[:], in0=hT[:], scalar=13.0 / 16.0, in1=conv[:, tiles, :], op0=ALU.add, op1=ALU.mult))
            wait(dve, e, ev["relu", b])
            ev["part", b, half] = S["dve"].after(dve.scalar_tensor_tensor(
                out=dt[b % 2][:, tiles, :], in0=hT[:], scalar=LOG1P_SMALL * (LOG1P_SMALL ** 2 / 3 - LOG1P_SMALL / 2 + 1),
                in1=dt[b % 2][:, tiles, :], op0=ALU.min, op1=ALU.add))

        def softplus_sum(b):
            wait(dve, ev["log", b])
            e = S["dve"].after(dve.tensor_scalar(yT[b % 2][:], yT[b % 2][:], log_small[:], 0.0, ALU.subtract, ALU.max))
            wait(dve, e, ev["part", b, 1])
            ev["dt", b] = S["dve"].after(dve.tensor_tensor(dt[b % 2][:], dt[b % 2][:], yT[b % 2][:], ALU.add))

        def skip(b):
            wait(dve, got("dt", b))
            for m in range(M):
                ev["skip", b] = S["dve"].after(dve.tensor_scalar(
                    yT[b % 2][:, m, :], xs[b % 2][:, m, :], d_skip[:, m:m + 1], None, ALU.mult))

        def scale_x(b):
            wait(pool, got("skip", b), got("xd_ps", b))
            ev["u", b] = S["pool"].after(pool.tensor_tensor(xs[b % 2][:], xs[b % 2][:], dt[b % 2][:], ALU.mult))

        def chunk(b, c):
            pair, q = c // 4, c % 4
            g = b * SLOTS + c
            da, h = dA[g % DA], hs[g % 3]
            wait(act, got("dt", b), got("scan", g - DA))
            for j in range(2):
                m = 2 * pair + j
                for n in range(Q):
                    ev["dA", g] = ev["dA_all", b] = S["dA"].after(act.activation(
                        da[:, j, n, 1:L], dt[b % 2][:, m, 1:L], ACT.Exp, scale=a_neg[:, m, q * Q + n:q * Q + n + 1]))
            spread = lambda mat: mat[:].unsqueeze(1).broadcast_to([P, 2, Q, L])
            wait(pool, got("u", b), got("bc", b, q), got("y_ps", g - 3))
            ev["dbx", g] = ev["dbx_all", b] = S["dbx"].after(pool.tensor_tensor(
                h[:], xs[b % 2][:, 2 * pair:2 * pair + 2, :].unsqueeze(2).broadcast_to([P, 2, Q, L]),
                spread(bmat[q]), ALU.mult))
            flat = h[:].rearrange("p j n l -> p (j n l)")
            wait(dve, ev["dA", g], ev["dbx", g])
            ev["scan", g] = S["scan"].after(dve.tensor_tensor_scan(
                flat, da[:].rearrange("p j n l -> p (j n l)"), flat, 0.0, ALU.mult, ALU.add))
            wait(dve, ev["scan", g], got("bc", b, q))
            ev["hc", g] = S["hc"].after(dve.tensor_tensor(h[:], h[:], spread(cmat[q]), ALU.mult))

        def sum_states(g):
            turn_of, q = g // 4, g % 4
            wait(pe, got("hc", g), got("y", turn_of - 2) if q == 0 else None)
            for n in range(Q):
                for j in range(2):
                    mm = pe.matmul(yps[:, turn_of % 2, j * L:(j + 1) * L], ident[:], hs[g % 3][:, j, n, :],
                                   start=(q == 0 and n == 0 and j == 0), stop=(q == 3 and n == Q - 1),
                                   skip_group_check=True)
            ev["y_ps", g] = S["y_ps"].after(mm)

        def add_y(b, pair):
            turn_of = b * PAIRS + pair
            dst = yT[b % 2][:, 2 * pair:2 * pair + 2, :]
            wait(dve, got("y_ps", 4 * turn_of + 3), got("skip", b))
            ev["y", turn_of] = S["evac"].after(dve.tensor_tensor(
                dst, dst, yps[:, turn_of % 2, 0:2 * L].rearrange("p (j l) -> p j l", j=2), ALU.add))

        def gate(b):
            wait(pool, got("y", b * PAIRS + PAIRS - 1), got("zs", b))
            ev["gated", b] = S["pool"].after(pool.tensor_tensor(yT[b % 2][:], yT[b % 2][:], zs[b % 2][:], ALU.mult))

        def out_proj(b, i, part):
            wait(pe, got("gated", b))
            bank = ev["o_bank", b, i] = ev["o_bank", b, i] if part else next_bank()
            for m in range(part * PAIRS, (part + 1) * PAIRS):
                mm = pe.matmul(work[0:TT, bank, :], yT[b % 2][:, m, i * TT:(i + 1) * TT], w_out[:, m, :],
                               start=(m == 0), stop=(m == M - 1))
            if part:
                ev["o_ps", b, i] = ev["o_ps", b] = S["work"].after(mm)

        def add_residual(b, i):
            bank = ev["o_bank", b, i]
            wait(dve, got("o_ps", b, i), got("res", b))
            e = freed[bank] = S["dve"].after(
                dve.tensor_tensor(xt[b % 3][:, i, :], xt[b % 3][:, i, :], work[0:TT, bank, :], ALU.add))
            wait(dve, e)
            e = S["dve"].after(dve.bn_stats(stats1[:, i, :], xt[b % 3][:, i, :]))
            wait(dve, e)
            e = S["dve"].after(dve.bn_aggr(mv1[:, 2 * b + i, :], stats1[:, i, :]))
            if i == 0:
                return
            ev["x1", b] = e
            wait(sp, e)
            ev["x1_stored", b] = S[f"xout{b % 3}"].after(
                sp.dma_start(x1_dram[b].rearrange("(i p) d -> p i d", p=TT), xt[b % 3][:]), 16)

        pieces = [w[r * P:(r + 1) * P, c * D:(c + 1) * D] for w in (t["w1"], t["w2"])
                  for r in range(w.shape[0] // P) for c in range(w.shape[1] // D)]
        assert len(pieces) <= B * SLOTS

        def load_piece(n):
            wait(sp, got("wsum", n - 2))
            ev["piece", n] = S[f"piece{n % 2}"].after(sp.dma_start(piece[n % 2][:], pieces[n]), 16)

        def sum_piece(n):
            wait(act, got("piece", n))
            ev["wsum", n] = S["act"].after(act.activation(
                piece[n % 2][:], piece[n % 2][:], ACT.Abs, accum_out=wsum[:, n:n + 1]))

        steps = [
            (-24, load_x), (-23, row_stats), (-21, guess_rsqrt), (-21, normalise), (-20, transpose_h), (-19, scale_hT),
            *((p - 18, lambda b, p=p: project(b, "x_ps", p)) for p in range(PAIRS)),
            *((p - 16, lambda b, p=p: last_tap(b, p)) for p in range(PAIRS)),
            *((p - 16, lambda b, p=p: older_taps(b, p)) for p in range(PAIRS)),
            *((p - 14, lambda b, p=p: project(b, "z_ps", p)) for p in range(PAIRS)),
            *((p - 12, lambda b, p=p: keep_z(b, p)) for p in range(PAIRS)),
            (-9, silus), (-9, x_dbl), (-8, keep_xd), (-7, dt_raw),
            (-5, softplus_tables), (-5, softplus_relu), (-5, lambda b: softplus_series(b, 0)), (-3, lambda b: square_half(b, 1)),
            (-3, lambda b: softplus_series(b, 1)), (-3, softplus_sum), (-3, skip), (-1, scale_x),
            *((q - 3, lambda b, q=q: spread_bc(b, q)) for q in range(4)),
            (SLOTS + 2, gate),
            *((SLOTS + 4 + 2 * i + part, lambda b, i=i, part=part: out_proj(b, i, part))
              for i in range(2) for part in range(2)),
            *((SLOTS + 6 + 2 * i, lambda b, i=i: add_residual(b, i)) for i in range(2)),
        ]
        for slot in range(-24, B * SLOTS + SLOTS):
            for b in range(B):
                at = slot - b * SLOTS
                if 1 <= at <= SLOTS:
                    sum_states(b * SLOTS + at - 1)
                if 0 <= at < SLOTS:
                    chunk(b, at)
                if 5 <= at <= SLOTS + 1 and at % 4 == 1:
                    add_y(b, (at - 5) // 4)
            for b in range(B):
                for offset, step in steps:
                    if slot - b * SLOTS == offset:
                        step(b)
            if slot >= 0:
                every = B * SLOTS // len(pieces)
                n = slot // every
                if n < len(pieces) and slot % every == 0:
                    load_piece(n)
                if n < len(pieces) and slot % every == every - 1:
                    sum_piece(n)
        for b in range(B - 3, B):
            wait(sp, ev["x1_stored", b])
        nc.all_engine_barrier()




def rstd_of_rows(nc, mem, mv, rstd, done_act, done_dve):
    rows, tiles, _ = mv.shape
    var_eps, guess, tmp = (mem.sbuf(n, [rows, tiles]) for n in ("row_var", "row_guess", "row_tmp"))
    e = done_dve.after(nc.vector.tensor_scalar(var_eps[:], mv[:, :, 1], EPS, None, ALU.add))
    wait(nc.scalar, e)
    wait(nc.scalar, done_act.after(nc.scalar.activation(guess[:], var_eps[:], ACT.Ln)))
    e = done_act.after(nc.scalar.activation(guess[:], guess[:], ACT.Exp, scale=-0.5))
    wait(nc.vector, e)
    return newton_rsqrt(nc.vector, done_dve, rstd[:], guess[:], var_eps[:], tmp[:])


def attention_phase(nc, t, x1_dram, x2_dram, mv1, mv2):
    B, D, KEYS = t["ctxT"].shape
    L = x1_dram.shape[1]
    TT = L // 2
    KD = D // P
    HEADS = 16
    DH = D // HEADS
    GROUP = P // DH
    GROUPS = HEADS // GROUP
    SLOTS = HEADS
    KC = 125
    CHUNKS = KEYS // KC
    HALF = KEYS // 2
    HPAD = HALF + HALF % 2
    KPAD = 2 * HPAD
    RING = GROUP + 1
    SCALE = float(DH) ** -0.5
    assert KC * CHUNKS == KEYS and CHUNKS % 2 == 0 and 2 * L <= BANK and HPAD <= BANK

    pe, act, dve, pool, sp = nc.tensor, nc.scalar, nc.vector, nc.gpsimd, nc.sync
    with ExitStack() as stack:
        mem = Memory(nc, stack, "b_")
        wk = [mem.sbuf(f"wk_{n}", [P, KD, D], F32R) for n in ("hi", "lo")]
        wv = [mem.sbuf(f"wv_{n}", [P, KD, D], F32R) for n in ("hi", "lo")]
        wq = mem.sbuf("wq", [P, KD, D])
        wo = mem.sbuf("wo", [P, KD, D])
        bq = mem.sbuf("bq", [P, KD])
        bk = mem.sbuf("bk", [P, KD])
        bv = mem.sbuf("bv", [P, D])
        bo = mem.sbuf("bo", [P, D])
        ident = mem.sbuf("ident", [P, P])
        mask = mem.sbuf("mask", [TT, 2, KEYS])
        rstd = mem.sbuf("rstd", [TT, 2 * B])
        raw = [mem.sbuf(f"raw{i}", [P, KPAD]) for i in range(2)]
        ctx = [mem.sbuf(f"ctx_{n}", [P, KD, KPAD], F32R) for n in ("hi", "lo")]
        k32 = mem.sbuf("k32", [P, HPAD])
        kT = [[mem.sbuf(f"kT{i}_{n}", [P, KPAD], F32R) for n in ("hi", "lo")] for i in range(2)]
        v = [mem.sbuf(f"v{i}", [KC, CHUNKS, D]) for i in range(2)]
        xt = [mem.sbuf(f"xt{i}", [TT, 2, D]) for i in range(2)]
        ln = mem.sbuf("ln", [TT, 2, D])
        stats = mem.sbuf("stats", [TT, 2, 6])
        hT = mem.sbuf("hT", [P, KD, L])
        q32 = mem.sbuf("q32", [P, L])
        qz = [[mem.sbuf(f"qz{i}_{n}", [P, GROUP, L], F32R) for n in ("hi", "lo")] for i in range(2)]
        sc = [mem.sbuf(f"sc{i}", [TT, 2, KEYS]) for i in range(2)]
        nmax = mem.sbuf("nmax", [TT, 2, HEADS])
        esum = mem.sbuf("esum", [TT, 2, HEADS])
        rsum = mem.sbuf("rsum", [TT, 2, GROUP])
        rwide = mem.sbuf("rwide", [TT, 2, GROUP, DH])
        pT = [mem.sbuf(f"pT{i}", [KC, CHUNKS, L]) for i in range(RING)]
        rb = mem.sbuf("rb", [P, L])
        oT = mem.sbuf("oT", [P, GROUPS, L])
        sps = mem.psum("sps", [P, 4, BANK])
        tps = mem.psum("tps", [P, 2, BANK])
        vps = mem.psum("vps", [P, BANK])
        ups = mem.psum("ups", [P, BANK])

        S = {n: mem.semaphore(n) for n in (
            "w", "raw0", "raw1", "xin0", "xin1", "xout0", "xout1", "const", "act", "dve", "pool",
            "unit", "s_ps", "ttr", "exp", "t_ps", "pt_act", "pt_dve", "pv", "ctx_hi", "ctx_lo", "k_hi", "k_lo",
            "q_hi", "q_lo", "free_act", "free_dve")}
        ev = {}

        def got(*key):
            assert key in ev or min(key[1:]) < 0, key
            return ev.get(key)

        for dst, src in (
            (wq[:], t["Wq"].rearrange("(k p) n -> p k n", p=P)), (wo[:], t["Wo"].rearrange("(k p) n -> p k n", p=P)),
            (bq[:], t["bq"]), (bk[:], t["bk"]), (ident[:], t["ident"]),
            (bv[:], t["bv"].partition_broadcast(P)), (bo[:], t["bo"].partition_broadcast(P)),
            (mask[:], t["mask"].rearrange("(i p) k -> p i k", p=TT)),
        ):
            weights = S["w"].after(act.dma_start(dst, src), 16)
        wait(dve, weights)
        S["const"].after(dve.tensor_scalar(bq[:], bq[:], SCALE, None, ALU.mult))
        S["const"].after(dve.tensor_scalar(mask[:], mask[:], NEG_INF_SCALE, None, ALU.mult))
        for i in range(2):
            for part in qz[i]:
                S["const"].after(dve.memset(part[:].bitcast(F32), 0.0))
            consts = S["const"].after(dve.memset(raw[i][:], 0.0))
        for engine in (pe, act, dve, pool, sp):
            wait(engine, weights, consts)
        rstd_ready = rstd_of_rows(nc, mem, mv1, rstd, S["act"], S["dve"])
        n = 0
        for w, name in ((wk, "Wk"), (wv, "Wv")):
            src = t[name].rearrange("(k p) n -> p k n", p=P)
            for k in range(KD):
                stage = raw[n % 2]
                wait(sp, got("raw_used", n - 2))
                e = S[f"raw{n % 2}"].after(sp.dma_start(stage[:, 0:D], src[:, k, :]), 16)
                wait(dve, e)
                e = S["ctx_hi"].after(dve.tensor_copy(w[0][:, k, :], stage[:, 0:D]))
                wait(pool, e)
                ev["raw_used", n] = S["ctx_lo"].after(
                    pool.tensor_tensor(w[1][:, k, :], stage[:, 0:D], w[0][:, k, :].bitcast(F32), ALU.subtract))
                n += 1
        split_weights = ev["raw_used", n - 1]
        wait(pe, split_weights)
        wait(dve, split_weights)
        for i in range(2):
            consts = S["const"].after(dve.memset(raw[i][:], 0.0))
        wait(sp, consts)
        TERMS = ((0, 0), (0, 1), (1, 0))

        def load_x1(b):
            wait(sp, got("x2_stored", b - 2))
            ev["x1", b] = S[f"xin{b % 2}"].after(
                sp.dma_start(xt[b % 2][:], x1_dram[b].rearrange("(i p) d -> p i d", p=TT)), 16)

        def normalise(b):
            wait(dve, got("x1", b), got("hT_ps", b - 1, 1), rstd_ready)
            for i in range(2):
                ev["ln", b] = S["dve"].after(dve.tensor_scalar(
                    ln[:, i, :], xt[b % 2][:, i, :], mv1[:, 2 * b + i, 0:1], rstd[:, 2 * b + i:2 * b + i + 1],
                    ALU.subtract, ALU.mult))
            wait(pool, ev["ln", b])
            for i in range(2):
                ev["res", b] = S["pool"].after(pool.tensor_tensor(xt[b % 2][:, i, :], xt[b % 2][:, i, :], bo[0:TT, :], ALU.add))

        last_free = [None]

        def unit_begins():
            wait(pe, last_free[0])

        def transpose_h(b, part):
            unit_begins()
            wait(pe, got("ln", b))
            for k2 in range(2):
                for i in range(2):
                    mm = pe.transpose(ups[:, k2 * L + i * TT:k2 * L + (i + 1) * TT],
                                      ln[:, i, (2 * part + k2) * P:(2 * part + k2 + 1) * P], ident[0:TT, 0:TT])
            ev["hT_ps", b, part] = S["unit"].after(mm)
            wait(act, ev["hT_ps", b, part], got("q_ps", b - 1, GROUPS - 1))
            ev["hT", b] = last_free[0] = S["free_act"].after(act.activation(
                hT[:, 2 * part:2 * part + 2, :], ups[:, 0:2 * L].rearrange("p (k l) -> p k l", k=2), ACT.Copy))

        def load_ctx(b):
            for k in range(KD):
                n = b * KD + k
                wait(sp, got("ctx_lo", n - 2))
                ev["raw", n] = S[f"raw{n % 2}"].after(
                    sp.dma_start(raw[n % 2][:, 0:KEYS], t["ctxT"][b].rearrange("(k p) s -> p k s", p=P)[:, k, :]), 16)
                wait(dve, ev["raw", n], got("k_ps", b - 1, GROUPS - 1, 1))
                ev["ctx_hi", n] = S["ctx_hi"].after(dve.tensor_copy(ctx[0][:, k, :], raw[n % 2][:]))
                wait(pool, ev["ctx_hi", n], got("k_ps", b - 1, GROUPS - 1, 1))
                ev["ctx_lo", n] = ev["ctx", b] = S["ctx_lo"].after(pool.tensor_tensor(
                    ctx[1][:, k, :], raw[n % 2][:], ctx[0][:, k, :].bitcast(F32), ALU.subtract))

        def project_k(b, g, half):
            G = b * GROUPS + g
            unit_begins()
            wait(pe, got("ctx", b))
            cols = slice(half * HPAD, (half + 1) * HPAD)
            for n, (i, j) in enumerate(TERMS):
                for k in range(KD):
                    mm = pe.matmul(ups[:, 0:HPAD], wk[i][:, k, g * P:(g + 1) * P], ctx[j][:, k, cols],
                                   start=(n == 0 and k == 0), stop=(n == 2 and k == KD - 1))
            ev["k_ps", b, g, half] = S["unit"].after(mm)
            wait(act, ev["k_ps", b, g, half], got("k_lo", 2 * G + half - 1))
            e = last_free[0] = S["free_act"].after(act.activation(
                k32[:], ups[:, 0:HPAD], ACT.Identity, bias=bk[:, g:g + 1]))
            hi, lo = kT[G % 2]
            wait(dve, e, got("s_ps", 4 * (G - 1) - 1))
            e = S["k_hi"].after(dve.tensor_copy(hi[:, cols], k32[:]))
            wait(pool, e, got("s_ps", 4 * (G - 1) - 1))
            ev["k_lo", 2 * G + half] = S["k_lo"].after(
                pool.tensor_tensor(lo[:, cols], k32[:], hi[:, cols].bitcast(F32), ALU.subtract))

        def project_v(b, c):
            unit_begins()
            wait(pe, got("ctx", b))
            for n, (i, j) in enumerate(TERMS):
                for k in range(KD):
                    mm = pe.matmul(ups[0:KC, :], ctx[i][:, k, c * KC:(c + 1) * KC], wv[j][:, k, :],
                                   start=(n == 0 and k == 0), stop=(n == 2 and k == KD - 1))
            e = S["unit"].after(mm)
            wait(dve, e, got("pv", b - 2, GROUPS - 1))
            ev["v", b] = last_free[0] = S["free_dve"].after(
                dve.tensor_tensor(v[b % 2][:, c, :], ups[0:KC, :], bv[0:KC, :], ALU.add))

        def project_q(b, g):
            G = b * GROUPS + g
            unit_begins()
            wait(pe, got("hT", b))
            for k in range(KD):
                mm = pe.matmul(ups[:, 0:L], wq[:, k, g * P:(g + 1) * P], hT[:, k, :], start=(k == 0), stop=(k == KD - 1))
            ev["q_ps", b, g] = S["unit"].after(mm)
            wait(act, ev["q_ps", b, g], got("q_lo", G - 1))
            e = last_free[0] = S["free_act"].after(act.activation(
                q32[:], ups[:, 0:L], ACT.Identity, bias=bq[:, g:g + 1], scale=SCALE))
            hi, lo = qz[G % 2]
            wait(dve, e, got("s_ps", 4 * (G - 1) - 1))
            for j in range(GROUP):
                rows = slice(j * DH, (j + 1) * DH)
                e = S["q_hi"].after(dve.tensor_copy(hi[rows, j, :], q32[rows, :]))
            wait(dve, e)
            for j in range(GROUP):
                rows = slice(j * DH, (j + 1) * DH)
                ev["q_lo", G] = S["q_lo"].after(dve.tensor_tensor(
                    lo[rows, j, :], q32[rows, :], hi[rows, j, :].bitcast(F32), ALU.subtract))

        def scores(n):
            G, j = n // GROUP, n % GROUP
            wait(pe, got("k_lo", 2 * G + 1), got("q_lo", G))
            for i in range(2):
                wait(pe, got("ttr", n - 1, i))
                for half in range(2):
                    for m, (a, c) in enumerate(TERMS):
                        mm = pe.matmul(sps[0:TT, 2 * i + half, 0:HPAD], qz[G % 2][a][:, j, i * TT:(i + 1) * TT],
                                       kT[G % 2][c][:, half * HALF:half * HALF + HPAD], start=(m == 0), stop=(m == 2))
                ev["s_ps", n, i] = ev["s_ps", n] = S["s_ps"].after(mm)

        def softmax(n):
            h = n % HEADS
            for i in range(2):
                wait(dve, got("s_ps", n, i), got("t_ps", n - 2))
                ev["ttr", n, i] = S["ttr"].after(dve.tensor_tensor_reduce(
                    out=sc[n % 2][:, i, :].rearrange("p (a k) -> p a k", a=2), in0=sps[0:TT, 2 * i:2 * i + 2, 0:HALF],
                    in1=mask[:, i, :].rearrange("p (a k) -> p a k", a=2), scale=-1.0, scalar=3.0e38,
                    op0=ALU.add, op1=ALU.min, accum_out=nmax[:, i, h:h + 1]))
            for i in range(2):
                wait(act, ev["ttr", n, i], got("rsum", n // GROUP - GROUPS))
                ev["exp", n] = S["exp"].after(act.activation(
                    sc[n % 2][:, i, :], sc[n % 2][:, i, :], ACT.Exp, scale=-1.0, bias=nmax[:, i, h:h + 1],
                    accum_out=esum[:, i, h:h + 1]))

        def transpose_p(n):
            wait(pe, got("exp", n))
            for pair in range(CHUNKS // 2):
                bank = (n * (CHUNKS // 2) + pair) % 2
                wait(pe, got("t_free", n * (CHUNKS // 2) + pair - 2))
                for c2 in range(2):
                    c = 2 * pair + c2
                    for i in range(2):
                        mm = pe.transpose(tps[0:KC, bank, c2 * L + i * TT:c2 * L + (i + 1) * TT],
                                          sc[n % 2][:, i, c * KC:(c + 1) * KC], ident[0:TT, 0:TT])
                e = ev["t_ps", n] = S["t_ps"].after(mm)
                dst = pT[n % RING][:, 2 * pair:2 * pair + 2, :]
                src = tps[0:KC, bank, 0:2 * L].rearrange("p (c l) -> p c l", c=2)
                G = (n - RING) // GROUP
                freed = got("pv", G // GROUPS, G % GROUPS) if n >= RING else None
                if bank == 0:
                    wait(act, e, freed)
                    ev["t_free", n * (CHUNKS // 2) + pair] = ev["pT_act", n] = S["pt_act"].after(
                        act.activation(dst, src, ACT.Copy))
                else:
                    wait(dve, e, freed)
                    ev["t_free", n * (CHUNKS // 2) + pair] = ev["pT_dve", n] = S["pt_dve"].after(
                        dve.tensor_copy(dst, src))

        def weigh_v(b, g):
            G = b * GROUPS + g
            first = G * GROUP
            wait(dve, got("exp", first + GROUP - 1), got("r_ps", G - 1))
            e = S["dve"].after(dve.reciprocal(rsum[:], esum[:, :, g * GROUP:(g + 1) * GROUP]))
            ev["rsum", G] = e
            wait(dve, e)
            for i in range(2):
                e = S["dve"].after(dve.tensor_copy(rwide[:, i], rsum[:, i, :].unsqueeze(2).broadcast_to([TT, GROUP, DH])))
            wait(pe, got("pT_act", first + GROUP - 1), got("pT_dve", first + GROUP - 1), got("v", b), got("oT", G - 1))
            for c in range(CHUNKS):
                for j in range(GROUP):
                    n = first + j
                    mm = pe.matmul(vps[j * DH:(j + 1) * DH, 0:L], v[b % 2][:, c, (g * GROUP + j) * DH:(g * GROUP + j + 1) * DH],
                                   pT[n % RING][:, c, :], start=(c == 0), stop=(c == CHUNKS - 1))
            ev["pv", b, g] = S["pv"].after(mm)
            unit_begins()
            wait(pe, e)
            for i in range(2):
                mm = pe.matmul(ups[:, i * TT:(i + 1) * TT], rwide[:, i].rearrange("p j d -> p (j d)"),
                               ident[0:TT, 0:TT], start=True, stop=True)
            ev["r_ps", G] = S["unit"].after(mm)
            wait(act, ev["r_ps", G], got("oT", G - 1))
            ev["rb", G] = last_free[0] = S["free_act"].after(act.activation(rb[:], ups[:, 0:L], ACT.Copy))

        def scale_o(b, g):
            G = b * GROUPS + g
            wait(dve, got("pv", b, g), got("rb", G), got("o_ps", b - 1))
            ev["oT", G] = S["dve"].after(dve.tensor_tensor(oT[:, g, :], vps[:, 0:L], rb[:], ALU.mult))

        def out_proj(b, i):
            unit_begins()
            wait(pe, got("oT", b * GROUPS + GROUPS - 1))
            for g in range(GROUPS):
                mm = pe.matmul(ups[0:TT, :], oT[:, g, i * TT:(i + 1) * TT], wo[:, g, :],
                               start=(g == 0), stop=(g == GROUPS - 1))
            ev["o_ps", b] = S["unit"].after(mm)
            wait(dve, ev["o_ps", b], got("res", b))
            e = last_free[0] = S["free_dve"].after(
                dve.tensor_tensor(xt[b % 2][:, i, :], xt[b % 2][:, i, :], ups[0:TT, :], ALU.add))
            wait(dve, e)
            e = S["dve"].after(dve.bn_stats(stats[:, i, :], xt[b % 2][:, i, :]))
            wait(dve, e)
            e = S["dve"].after(dve.bn_aggr(mv2[:, 2 * b + i, :], stats[:, i, :]))
            if i == 1:
                wait(sp, e)
                ev["x2_stored", b] = S[f"xout{b % 2}"].after(
                    sp.dma_start(x2_dram[b].rearrange("(i p) d -> p i d", p=TT), xt[b % 2][:]), 16)

        steps = [
            (-9, load_x1), (-7, normalise), (-6, load_ctx),
            (-5, lambda b: transpose_h(b, 0)), (-4, lambda b: transpose_h(b, 1)),
            *((4 * g - 4 + half, lambda b, g=g, half=half: project_k(b, g, half))
              for g in range(GROUPS) for half in range(2)),
            *((4 * g - 2, lambda b, g=g: project_q(b, g)) for g in range(GROUPS)),
            (-3, lambda b: project_v(b, 0)), (-2, lambda b: project_v(b, 1)), (-2, lambda b: project_v(b, 2)),
            (-1, lambda b: project_v(b, 3)), (-1, lambda b: project_v(b, 4)), (0, lambda b: project_v(b, 5)),
            *((4 * g + 5, lambda b, g=g: weigh_v(b, g)) for g in range(GROUPS)),
            *((4 * g + 6, lambda b, g=g: scale_o(b, g)) for g in range(GROUPS)),
            (SLOTS + 3, lambda b: out_proj(b, 0)), (SLOTS + 4, lambda b: out_proj(b, 1)),
        ]
        for slot in range(-9, B * SLOTS + 5):
            if 0 <= slot < B * SLOTS:
                scores(slot)
                softmax(slot)
            for b in range(B):
                for offset, step in steps:
                    if slot - b * SLOTS == offset:
                        step(b)
            if 1 <= slot <= B * SLOTS:
                transpose_p(slot - 1)
        for b in range(B - 2, B):
            wait(sp, ev["x2_stored", b])
        nc.all_engine_barrier()


def ffn_phase(nc, t, x2_dram, out, mv2, wsum):
    B, L, D = x2_dram.shape
    TT = L // 2
    TILES = 4
    T = TILES * TT
    STEPS = B * L // T
    KD = D // P
    F = t["w1"].shape[0]
    FT = F // P
    LAG = 2
    assert T <= BANK and D <= BANK and wsum.shape[1] == FT + F // D * KD

    pe, act, dve, pool, sp = nc.tensor, nc.scalar, nc.vector, nc.gpsimd, nc.sync
    with ExitStack() as stack:
        mem = Memory(nc, stack, "c_")
        s1 = mem.sbuf("s1", [P, KD, F], F32R)
        s2 = mem.sbuf("s2", [P, FT, D], F32R)
        raw = [mem.sbuf(f"raw{i}", [P, F]) for i in range(2)]
        b1 = mem.sbuf("b1", [P, FT])
        b2 = mem.sbuf("b2", [P, D])
        ident = mem.sbuf("ident", [P, P])
        ones = mem.sbuf("ones", [P, P])
        alpha1 = mem.sbuf("alpha1", [P, FT])
        alpha2 = mem.sbuf("alpha2", [P, KD])
        diag = mem.sbuf("diag", [P, KD, P])
        alpha2_row = mem.sbuf("alpha2_row", [P, D])
        rstd = mem.sbuf("rstd", [TT, 2 * B])
        xt = [mem.sbuf(f"xt{i}", [TT, TILES, D]) for i in range(3)]
        ln = mem.sbuf("ln", [TT, TILES, D])
        hT = [[mem.sbuf(f"hT{i}_{n}", [P, KD, T], F32R) for n in ("hi", "lo")] for i in range(2)]
        g32 = [mem.sbuf(f"g32_{i}", [P, T]) for i in range(2)]
        gT = [[mem.sbuf(f"gT{i}_{n}", [P, T], F32R) for n in ("hi", "lo")] for i in range(LAG + 1)]
        prod = [mem.sbuf(f"prod{i}", [TT, D]) for i in range(2)]
        tps = mem.psum("tps", [P, BANK])
        fps = mem.psum("fps", [P, 3, BANK])
        ops = mem.psum("ops", [P, TILES, BANK])

        S = {n: mem.semaphore(n) for n in (
            "w", "raw0", "raw1", "xin0", "xin1", "xin2", "xout0", "xout1", "xout2", "const", "act", "dve",
            "sign1", "sign2", "pool", "t_ps", "h_hi", "h_lo", "f_ps", "gelu", "g_hi", "g_lo", "o_ps", "prod", "sum")}
        ev = {}

        def got(*key):
            assert key in ev or min(key[1:]) < 0, key
            return ev.get(key)

        for dst, src in ((b1[:], t["b1"]), (ident[:], t["ident"]), (b2[:], t["b2"].partition_broadcast(P))):
            weights = S["w"].after(act.dma_start(dst, src), 16)
        rstd_ready = rstd_of_rows(nc, mem, mv2, rstd, S["act"], S["dve"])

        w1T = t["w1T"].rearrange("(k p) f -> p k f", p=P)
        w2T = t["w2T"].rearrange("(a c p) d -> a p c d", p=P, c=F // D)
        loads = [(w1T[:, k, :], s1[:, k, :], "sign1") for k in range(KD)]
        loads += [(w2T[a], s2[:, a * (F // D):(a + 1) * (F // D), :], "sign2") for a in range(KD)]
        for n, (src, dst, name) in enumerate(loads):
            stage = raw[n % 2][:] if name == "sign1" else raw[n % 2][:].rearrange("p (c d) -> p c d", d=D)
            wait(sp, got("sign", n - 2))
            e = S[f"raw{n % 2}"].after(sp.dma_start(stage, src), 16)
            wait(act, e)
            ev["sign", n] = S[name].after(act.activation(dst, stage, ACT.Sign))
        signs1, signs2 = ev["sign", KD - 1], ev["sign", 2 * KD - 1]

        for engine in (dve, pe, act, pool):
            wait(engine, weights)
        alpha1_ready = S["const"].after(dve.tensor_scalar(alpha1[:], wsum[:, 0:FT], 1.0 / D, None, ALU.mult))
        e = S["const"].after(dve.tensor_reduce(
            alpha2[:], wsum[:, FT:].rearrange("p (r c) -> p r c", c=F // D), AX_X, ALU.add))
        wait(dve, e)
        for k in range(KD):
            S["const"].after(dve.tensor_scalar(diag[:, k, :], ident[:], alpha2[:, k:k + 1], 1.0 / F, ALU.mult, ALU.mult))
        e = S["const"].after(dve.memset(ones[:], 1.0))
        wait(pe, e)
        for k in range(KD):
            mm = pe.matmul(tps[:, k * P:(k + 1) * P], ones[:], diag[:, k, :], start=True, stop=True)
        e = S["t_ps"].after(mm)
        wait(dve, e)
        alpha2_ready = S["const"].after(dve.tensor_copy(alpha2_row[:], tps[:, 0:D]))
        wait(pe, alpha2_ready)
        wait(act, alpha1_ready)

        x2_tiles = x2_dram.rearrange("b (i p) d -> p (b i) d", p=TT)
        out_tiles = out.rearrange("b (i p) d -> p (b i) d", p=TT)

        def load_x2(c):
            wait(sp, got("stored", c - 3))
            ev["x2", c] = S[f"xin{c % 3}"].after(
                sp.dma_start(xt[c % 3][:], x2_tiles[:, TILES * c:TILES * (c + 1), :]), 16)

        def normalise(c):
            wait(dve, got("x2", c), got("h_ps", c - 1, KD - 1), rstd_ready)
            for i in range(TILES):
                n = TILES * c + i
                ev["ln", c] = S["dve"].after(dve.tensor_scalar(
                    ln[:, i, :], xt[c % 3][:, i, :], mv2[:, n, 0:1], rstd[:, n:n + 1], ALU.subtract, ALU.mult))
            wait(pool, ev["ln", c])
            for i in range(TILES):
                ev["res", c] = S["pool"].after(pool.tensor_tensor(
                    xt[c % 3][:, i, :], xt[c % 3][:, i, :], b2[0:TT, :], ALU.add))

        def transpose_h(c, k):
            wait(pe, got("ln", c), got("h_lo", c, k - 1) if k else got("h_lo", c - 1, KD - 1))
            for i in range(TILES):
                mm = pe.transpose(tps[:, i * TT:(i + 1) * TT], ln[:, i, k * P:(k + 1) * P], ident[0:TT, 0:TT])
            ev["h_ps", c, k] = S["t_ps"].after(mm)
            hi, lo = hT[c % 2]
            used = got("f_ps", (c - 2) * FT + FT - 1)
            wait(act, ev["h_ps", c, k], used)
            e = S["h_hi"].after(act.activation(hi[:, k, :], tps[:, 0:T], ACT.Copy))
            wait(dve, e, used)
            ev["h_lo", c, k] = S["h_lo"].after(
                dve.tensor_tensor(lo[:, k, :], tps[:, 0:T], hi[:, k, :].bitcast(F32), ALU.subtract))

        def hidden(n):
            c, f = n // FT, n % FT
            wait(pe, got("h_lo", c, KD - 1), signs1, got("gelu", n - 3))
            for k in range(KD):
                for part in range(2):
                    mm = pe.matmul(fps[:, n % 3, 0:T], s1[:, k, f * P:(f + 1) * P], hT[c % 2][part][:, k, :],
                                   start=(k == 0 and part == 0), stop=(k == KD - 1 and part == 1))
            ev["f_ps", n] = S["f_ps"].after(mm)
            wait(act, ev["f_ps", n], got("g_lo", n - 2))
            ev["gelu", n] = S["gelu"].after(act.activation(
                g32[n % 2][:], fps[:, n % 3, 0:T], ACT.Gelu, scale=alpha1[:, f:f + 1], bias=b1[:, f:f + 1]))
            hi, lo = gT[n % (LAG + 1)]
            wait(dve, ev["gelu", n], got("o_ps", n - LAG - 1))
            e = S["g_hi"].after(dve.tensor_copy(hi[:], g32[n % 2][:]))
            wait(pool, e, got("o_ps", n - LAG - 1))
            ev["g_lo", n] = S["g_lo"].after(pool.tensor_tensor(lo[:], g32[n % 2][:], hi[:].bitcast(F32), ALU.subtract))

        def second(n):
            c, f = n // FT, n % FT
            wait(pe, got("g_lo", n), signs2)
            for i in range(TILES):
                if f == 0:
                    wait(pe, got("prod", c - 1, i))
                for part in range(2):
                    mm = pe.matmul(ops[0:TT, i, :], gT[n % (LAG + 1)][part][:, i * TT:(i + 1) * TT], s2[:, f, :],
                                   start=(f == 0 and part == 0), stop=(f == FT - 1 and part == 1))
                if f == FT - 1:
                    ev["o_tile", c, i] = S["o_ps"].after(mm)
            ev["o_ps", n] = S["o_ps"].after(mm) if f < FT - 1 else ev["o_tile", c, TILES - 1]

        def finish(c):
            for i in range(TILES):
                m = c * TILES + i
                wait(dve, ev["o_tile", c, i], got("sum", m - 2))
                ev["prod", c, i] = S["prod"].after(
                    dve.tensor_tensor(prod[m % 2][:], ops[0:TT, i, :], alpha2_row[0:TT, :], ALU.mult))
                wait(pool, ev["prod", c, i], got("res", c))
                ev["sum", m] = S["sum"].after(
                    pool.tensor_tensor(xt[c % 3][:, i, :], xt[c % 3][:, i, :], prod[m % 2][:], ALU.add))
            wait(sp, ev["sum", m])
            ev["stored", c] = S[f"xout{c % 3}"].after(
                sp.dma_start(out_tiles[:, TILES * c:TILES * (c + 1), :], xt[c % 3][:]), 16)

        steps = [(-12, load_x2), (-8, normalise), *((k - 6, lambda c, k=k: transpose_h(c, k)) for k in range(KD)),
                 (FT + LAG - 1, finish)]
        for slot in range(-12, STEPS * FT + LAG + 1):
            if 0 <= slot < STEPS * FT:
                hidden(slot)
            if LAG <= slot < STEPS * FT + LAG:
                second(slot - LAG)
            for c in range(STEPS):
                for offset, step in steps:
                    if slot - c * FT == offset:
                        step(c)
        for c in range(STEPS - 3, STEPS):
            wait(sp, ev["stored", c])


def decoder_layer(nc, t, out):
    B, L, D = t["x"].shape
    TT = L // 2
    N = t["A_log"].shape[1]
    F = t["w1"].shape[0]
    x1_dram = nc.dram_tensor("x1_scratch", (B, L, D), F32).ap()
    x2_dram = nc.dram_tensor("x2_scratch", (B, L, D), F32).ap()
    bc_dram = nc.dram_tensor("bc_scratch", (B, 2 * N, L), F32).ap()
    with ExitStack() as stack:
        mem = Memory(nc, stack, "")
        mv1 = mem.sbuf("mv1", [TT, 2 * B, 2])
        mv2 = mem.sbuf("mv2", [TT, 2 * B, 2])
        wsum = mem.sbuf("wsum", [P, F // P + F // D * (D // P)])
        mamba_phase(nc, t, x1_dram, bc_dram, mv1, wsum)
        attention_phase(nc, t, x1_dram, x2_dram, mv1, mv2)
        ffn_phase(nc, t, x2_dram, out, mv2, wsum)


def kernel(**inputs):
    import concourse.bacc as bacc
    from concourse.bass_utils import run_bass_kernel_spmd

    def columns(a):
        return np.asarray(a).reshape(-1, P).T

    i = {k: np.asarray(v) for k, v in inputs.items()}
    mamba = {k: i["L0_attn_" + k] for k in ("W_in", "conv_w", "W_x", "W_dt", "A_log", "W_out")}
    mamba |= {k: columns(i["L0_attn_" + k]) for k in ("norm_w", "conv_b", "b_dt", "D")}
    xattn = {k: i["L0_xattn_" + k] for k in ("Wq", "Wk", "Wv", "Wo", "bv", "bo")}
    xattn |= {k: columns(i["L0_xattn_" + k]) for k in ("bq", "bk")}
    ffn = {"w1": i["L0_ffn_w1"], "w2": i["L0_ffn_w2"], "w1T": i["L0_ffn_w1"].T, "w2T": i["L0_ffn_w2"].T,
           "b1": columns(i["L0_ffn_b1"]), "b2": i["L0_ffn_b2"]}
    arrays = {"x": i["x"], "ctxT": i["ctx_1024"].transpose(0, 2, 1), "mask": i["mask_1x1xSxS2_fk1"][0, 0],
              "ident": np.eye(P, dtype=np.float32), **mamba, **xattn, **ffn}
    arrays = {k: np.ascontiguousarray(a) for k, a in arrays.items()}

    nc = bacc.Bacc("TRN2", target_bir_lowering=False, num_devices=1)
    t = {k: nc.dram_tensor(k + "_dram", a.shape, mybir.dt.from_np(a.dtype), kind="ExternalInput").ap()
         for k, a in arrays.items()}
    out = nc.dram_tensor("out_dram", i["x"].shape, F32, kind="ExternalOutput").ap()
    decoder_layer(nc, t, out)
    result = run_bass_kernel_spmd(nc, [{k + "_dram": a for k, a in arrays.items()}], core_ids=[0])
    return result.results[0]["out_dram"]
```

```python
from contextlib import ExitStack

import numpy as np

import concourse.bass as bass
from concourse import mybir

P = 128
F32 = mybir.dt.float32
F32R = mybir.dt.float32r
ALU = mybir.AluOpType
ACT = mybir.ActivationFunctionType
AX_X = mybir.AxisListType.X
BANK = 512
EPS = 1e-5
NEG_INF_SCALE = -1e9
LOG1P_SMALL = 2.0 ** -8


class Counted:

    def __init__(self, sem):
        self.sem, self.value = sem, 0

    def after(self, instruction, by=1):
        instruction.then_inc(self.sem, by)
        self.value += by
        return self.sem, self.value


def wait(engine, *events):
    for event in events:
        if event is not None:
            engine.wait_ge(*event)


class Memory:

    def __init__(self, nc, stack, prefix):
        self.nc, self.stack, self.prefix = nc, stack, prefix

    def sbuf(self, name, shape, dtype=F32):
        return self.stack.enter_context(self.nc.sbuf_tensor(self.prefix + name, shape, dtype))

    def arena(self, name, shape):
        self.sbuf(name, shape)
        return self.nc.sbuf_base - int(np.prod(shape[1:])) * 4

    def inside(self, name, shape, start, dtype=F32):
        return self.nc.alloc_sbuf_tensor_at(self.prefix + name, shape, dtype, offset=start)

    def psum(self, name, shape):
        return self.stack.enter_context(self.nc.psum_tensor(self.prefix + name, shape, F32))

    def semaphore(self, name):
        return Counted(self.stack.enter_context(self.nc.semaphore(self.prefix + name)))


class Shared:

    def __init__(self, mem, D, F):
        start = mem.arena("shared", [P, D // P, F])
        row = 4 * F

        def parts(name, first):
            return [mem.inside(f"{name}_{n}", [P, D // P, D], start + (first + r) * row, F32R)
                    for n, r in (("hi", 1), ("lo", 0))]

        self.w_in = mem.inside("w_in", [P, D // P, F], start)
        self.raw_k, self.k = mem.inside("raw_k", [P, D // P, D], start), parts("wk", 0)
        self.raw_v, self.v = mem.inside("raw_v", [P, D // P, D], start + 2 * row), parts("wv", 2)
        self.raw_1, self.s1 = mem.inside("raw_w1", [P, D // P, F], start), mem.inside("s1", [P, D // P, F], start, F32R)


def newton_rsqrt(dve, done, out, guess, value, tmp):
    wait(dve, done.after(dve.tensor_tensor(tmp, guess, guess, ALU.mult)))
    wait(dve, done.after(dve.tensor_tensor(tmp, tmp, value, ALU.mult)))
    wait(dve, done.after(dve.tensor_scalar(tmp, tmp, -0.5, 1.5, ALU.mult, ALU.add)))
    event = done.after(dve.tensor_tensor(out, tmp, guess, ALU.mult))
    wait(dve, event)
    return event


def mamba_phase(nc, t, x1_dram, bc_dram, mv1, wsum, shared):
    B, L, D = t["x"].shape
    TT = L // 2
    KD = D // P
    DI = t["W_out"].shape[0]
    M = DI // P
    R = t["W_dt"].shape[0]
    N = t["A_log"].shape[1]
    Q = N // 4
    TAPS = t["conv_w"].shape[1]
    DA = 2
    PAIRS = M // 2
    SLOTS = 4 * PAIRS
    assert TT <= P and 2 * L <= BANK and R + 2 * N <= P

    pe, act, dve, pool, sp = nc.tensor, nc.scalar, nc.vector, nc.gpsimd, nc.sync
    with ExitStack() as stack:
        mem = Memory(nc, stack, "a_")
        w_in = shared.w_in
        w_out = mem.sbuf("w_out", [P, M, D])
        w_x = mem.sbuf("w_x", [P, M, R + 2 * N])
        w_dt = mem.sbuf("w_dt", [R, DI])
        a_neg = mem.sbuf("a_neg", [P, M, N])
        norm_w = mem.sbuf("norm_w", [P, KD])
        conv_w = mem.sbuf("conv_w", [P, M, TAPS])
        conv_b = mem.sbuf("conv_b", [P, M])
        b_dt = mem.sbuf("b_dt", [P, M])
        d_skip = mem.sbuf("d_skip", [P, M])
        ident = mem.sbuf("ident", [P, P])
        log_small = mem.sbuf("log_small", [P, 1])
        series_bias = mem.sbuf("series_bias", [P, 1])
        xt = [mem.sbuf(f"xt{i}", [TT, 2, D]) for i in range(3)]
        h = mem.sbuf("h", [TT, 2, D])
        stats = mem.sbuf("stats", [TT, 2, 6])
        mv = mem.sbuf("mv", [TT, 2, 2])
        squares = mem.sbuf("squares", [TT, 2, 2])
        guess = mem.sbuf("guess", [TT, 2, 2])
        ntmp = mem.sbuf("ntmp", [TT, 2, 2])
        rsqrt = mem.sbuf("rsqrt", [TT, 2, 2])
        gain = mem.sbuf("gain", [TT, 2, 2])
        stats1 = mem.sbuf("stats1", [TT, 2, 6])
        hT = mem.sbuf("hT", [P, KD, L])
        conv = mem.sbuf("conv", [P, M, L])
        xs = [mem.sbuf(f"xs{i}", [P, M, L]) for i in range(2)]
        zs = [mem.sbuf(f"zs{i}", [P, M, L]) for i in range(2)]
        dt = [mem.sbuf(f"dt{i}", [P, M, L]) for i in range(2)]
        yT = [mem.sbuf(f"yT{i}", [P, M, L]) for i in range(2)]
        piece = [mem.sbuf(f"piece{i}", [P, D]) for i in range(2)]
        xd = mem.sbuf("xd", [R + 2 * N, L])
        bmat = [mem.sbuf(f"bmat{i}", [P, Q, L]) for i in range(4)]
        cmat = [mem.sbuf(f"cmat{i}", [P, Q, L]) for i in range(4)]
        dA = [mem.sbuf(f"dA{i}", [P, 2, Q, L]) for i in range(DA)]
        hs = [mem.sbuf(f"hs{i}", [P, 2, Q, L]) for i in range(3)]
        work = mem.psum("work", [P, 6, BANK])
        yps = mem.psum("yps", [P, 2, BANK])

        S = {n: mem.semaphore(n) for n in (
            "w", "w_in0", "w_in1", "w_out", "wk", "wv", "split", "xin0", "xin1", "xin2", "xout0", "xout1", "xout2", "piece0", "piece1", "bcst", "bc0", "bc1", "bc2", "bc3",
            "const", "dve", "act", "pool", "work", "y_ps",
            "dA", "dbx", "u", "scan", "hc", "evac", "xs_done", "zs_done")}

        for dst, src in (
            (a_neg[:], t["A_log"].rearrange("(m p) n -> p m n", p=P)), (ident[:], t["ident"]),
            (norm_w[:], t["norm_w"]), (conv_w[:], t["conv_w"].rearrange("(m p) k -> p m k", p=P)),
            (conv_b[:], t["conv_b"]), (b_dt[:], t["b_dt"]), (d_skip[:], t["D"]), (w_dt[:], t["W_dt"]),
            (w_x[:], t["W_x"].rearrange("(m p) r -> p m r", p=P)),
        ):
            weights = S["w"].after(act.dma_start(dst, src), 16)
        w_out_loaded = S["w_out"].after(act.dma_start(w_out[:], t["W_out"].rearrange("(m p) d -> p m d", p=P)), 16)
        act.preload_act_table_set("natural_log_exp_and_others")
        wait(act, weights)
        e = S["act"].after(act.activation(a_neg[:], a_neg[:], ACT.Exp))
        wait(dve, e)
        S["const"].after(dve.tensor_scalar(a_neg[:], a_neg[:], -1.0, None, ALU.mult))
        S["const"].after(dve.memset(series_bias[:], -(3.0 ** 0.5) / 4.0))
        e = S["const"].after(dve.memset(log_small[:], LOG1P_SMALL))
        wait(act, e)
        e = S["act"].after(act.activation(log_small[:], log_small[:], ACT.Ln, bias=1.0))
        wait(dve, e)
        for i in range(DA):
            consts = S["const"].after(dve.memset(dA[i][:, :, :, 0:1], 0.0))
        for engine in (pe, act, dve, pool):
            wait(engine, weights, consts)

        ev = {}

        def got(*key):
            assert key in ev or min(key[1:]) < 0, key
            return ev.get(key)

        def load_x(b):
            wait(sp, got("x1_stored", b - 3))
            ev["x", b] = S[f"xin{b % 3}"].after(
                sp.dma_start(xt[b % 3][:], t["x"][b].rearrange("(i p) d -> p i d", p=TT)), 16)

        load_x(0)
        k_in = t["W_in"].rearrange("(k p) m -> p k m", p=P)
        w_in_loaded = {}
        for i, name in enumerate(("x_ps", "z_ps")):
            for k in range(KD):
                w_in_loaded[name] = S[f"w_in{i}"].after(
                    sp.dma_start(w_in[:, k, i * DI:(i + 1) * DI], k_in[:, k, i * DI:(i + 1) * DI]), 16)

        def row_stats(b):
            wait(dve, got("x", b))
            for i in range(2):
                e = S["dve"].after(dve.bn_stats(stats[:, i, :], xt[b % 3][:, i, :]))
            wait(dve, e)
            for i in range(2):
                e = S["dve"].after(dve.bn_aggr(mv[:, i, :], stats[:, i, :]))
            wait(dve, e)
            e = S["dve"].after(dve.tensor_scalar(squares[:, 0, :], mv[:, :, 1], EPS, None, ALU.add))
            wait(dve, e)
            e = S["dve"].after(dve.reciprocal(ntmp[:, 0, :], squares[:, 0, :]))
            wait(dve, e)
            e = S["dve"].after(dve.tensor_tensor(ntmp[:, 1, :], ntmp[:, 0, :], mv[:, :, 1], ALU.mult))
            wait(dve, e)
            ev["squares", b] = S["dve"].after(dve.tensor_scalar(squares[:, 1, :], ntmp[:, 1, :], EPS, None, ALU.add))

        def guess_rsqrt(b):
            wait(act, got("squares", b))
            e = S["act"].after(act.activation(guess[:], squares[:], ACT.Ln))
            wait(act, e)
            ev["guess", b] = S["act"].after(act.activation(guess[:], guess[:], ACT.Exp, scale=-0.5))

        def normalise(b):
            wait(dve, got("guess", b))
            newton_rsqrt(dve, S["dve"], rsqrt[:], guess[:], squares[:], ntmp[:])
            S["dve"].after(dve.tensor_tensor(ntmp[:, 0, :], rsqrt[:, 0, :], rsqrt[:, 1, :], ALU.mult))
            S["dve"].after(dve.tensor_scalar(gain[:, 0, :], rsqrt[:, 0, :], 1.0, None, ALU.add))
            e = S["dve"].after(dve.tensor_tensor(gain[:, 1, :], rsqrt[:, 0, :], mv[:, :, 0], ALU.mult))
            wait(dve, e, got("hT_read", b - 1))
            for i in range(2):
                e = ev["h", b] = S["dve"].after(dve.tensor_scalar(
                    h[:, i, :], xt[b % 3][:, i, :], mv[:, i, 0:1], ntmp[:, 0, i:i + 1], ALU.subtract, ALU.mult))
            wait(dve, e)
            for i in range(2):
                ev["res", b] = S["dve"].after(dve.tensor_scalar(
                    xt[b % 3][:, i, :], xt[b % 3][:, i, :], gain[:, 0, i:i + 1], gain[:, 1, i:i + 1],
                    ALU.mult, ALU.subtract))

        freed = [None] * 6
        turn = [0]

        def next_bank():
            bank = turn[0] % 6
            turn[0] += 1
            wait(pe, freed[bank])
            return bank

        def transpose_h(b):
            wait(pe, got("h", b))
            for half in range(2):
                bank = ev["hT_bank", b, half] = next_bank()
                for k in range(2 * half, 2 * half + 2):
                    for i in range(2):
                        col = (k % 2) * L + i * TT
                        mm = pe.transpose(work[:, bank, col:col + TT], h[:, i, k * P:(k + 1) * P], ident[0:TT, 0:TT])
                ev["hT_ps", b, half] = ev["hT_read", b] = S["work"].after(mm)

        def scale_hT(b):
            for k in range(KD):
                bank = ev["hT_bank", b, k // 2]
                wait(dve, got("hT_ps", b, k // 2), got("part", b - 1, 1))
                ev["hT", b] = freed[bank] = S["dve"].after(dve.tensor_scalar(
                    hT[:, k, :], work[:, bank, (k % 2) * L:(k % 2 + 1) * L], norm_w[:, k:k + 1], None, ALU.mult))

        def project(b, name, pair):
            first = 2 * pair + (M if name == "z_ps" else 0)
            wait(pe, got("hT", b), w_in_loaded[name])
            bank = ev[name + "_bank", b, pair] = next_bank()
            for j in range(2):
                for k in range(KD):
                    mm = pe.matmul(work[:, bank, j * L:(j + 1) * L], w_in[:, k, (first + j) * P:(first + j + 1) * P],
                                   hT[:, k, :], start=(k == 0), stop=(k == KD - 1))
            ev[name, b, pair] = S["work"].after(mm)

        def keep_z(b, pair):
            bank = ev["z_ps_bank", b, pair]
            wait(act, got("z_ps", b, pair), got("gated", b - 2))
            ev["z", b] = freed[bank] = S["act"].after(act.activation(
                zs[b % 2][:, 2 * pair:2 * pair + 2, :],
                work[:, bank, 0:2 * L].rearrange("p (j l) -> p j l", j=2), ACT.Copy))

        def last_tap(b, pair):
            bank = ev["x_ps_bank", b, pair]
            wait(act, got("x_ps", b, pair), got("dt", b - 1))
            for j in range(2):
                m = 2 * pair + j
                e = S["act"].after(act.activation(conv[:, m, :], work[:, bank, j * L:(j + 1) * L], ACT.Identity,
                                                  scale=conv_w[:, m, TAPS - 1:TAPS], bias=conv_b[:, m:m + 1]))
            ev["tap", b, pair] = e

        def older_taps(b, pair):
            bank = ev["x_ps_bank", b, pair]
            wait(dve, got("tap", b, pair))
            for back in range(1, TAPS):
                for j in range(2):
                    m = 2 * pair + j
                    e = S["dve"].after(dve.scalar_tensor_tensor(
                        out=conv[:, m, back:], in0=work[:, bank, j * L:(j + 1) * L - back],
                        scalar=conv_w[:, m, TAPS - 1 - back:TAPS - back], in1=conv[:, m, back:],
                        op0=ALU.mult, op1=ALU.add))
                wait(dve, e)
            ev["conv", b, pair] = freed[bank] = e

        def silus(b):
            wait(act, *(got("conv", b, p) for p in range(PAIRS)), got("z", b), got("dbx_all", b - 2))
            ev["xs", b] = S["xs_done"].after(act.activation(xs[b % 2][:], conv[:], ACT.Silu))
            ev["zs", b] = S["zs_done"].after(act.activation(zs[b % 2][:], zs[b % 2][:], ACT.Silu))
            act.preload_act_table_set("natural_log_exp_and_others")

        def x_dbl(b):
            wait(pe, got("xs", b))
            bank = ev["xd_bank", b] = next_bank()
            for m in range(M):
                mm = pe.matmul(work[0:R + 2 * N, bank, 0:L], w_x[:, m, :], xs[b % 2][:, m, :],
                               start=(m == 0), stop=(m == M - 1))
            ev["xd_ps", b] = S["work"].after(mm)

        def keep_xd(b):
            bank = ev["xd_bank", b]
            wait(dve, got("xd_ps", b), got("dt_ps", b - 1, PAIRS - 1), got("bc_stored", b - 1))
            ev["xd", b] = freed[bank] = S["dve"].after(dve.tensor_copy(xd[:], work[0:R + 2 * N, bank, 0:L]))
            wait(sp, ev["xd", b])
            ev["bc_stored", b] = S["bcst"].after(sp.dma_start(bc_dram[b], xd[R:R + 2 * N, :]), 16)

        def spread_bc(b, q):
            wait(sp, got("bc_stored", b), got("hc", b * SLOTS + q - 4))
            for dst, row in ((bmat[q], q * Q), (cmat[q], N + q * Q)):
                src = bc_dram[b, row:row + Q, :].partition_broadcast(P)
                ev["bc", b, q] = S[f"bc{q}"].after(sp.dma_start(dst[:], src), 16)

        def dt_raw(b):
            wait(pe, got("xd", b))
            for pair in range(PAIRS):
                bank = ev["dt_bank", b, pair] = next_bank()
                for j in range(2):
                    m = 2 * pair + j
                    mm = pe.matmul(work[:, bank, j * L:(j + 1) * L], w_dt[:, m * P:(m + 1) * P], xd[0:R, :],
                                   start=True, stop=True)
                ev["dt_ps", b, pair] = S["work"].after(mm)

        def softplus_tables(b):
            for pair in range(PAIRS):
                wait(act, got("dt_ps", b, pair), got("xs", b))
                bank = ev["dt_bank", b, pair]
                for j in range(2):
                    m = 2 * pair + j
                    e = ev["abs", b, pair] = S["act"].after(act.activation(
                        conv[:, m, :], work[:, bank, j * L:(j + 1) * L], ACT.Abs, bias=b_dt[:, m:m + 1]))
            wait(act, e)
            e = S["act"].after(act.activation(conv[:], conv[:], ACT.Exp, scale=-1.0))
            wait(act, e, got("z_ps", b, PAIRS - 1), got("o_ps", b - 2))
            ev["log", b] = S["act"].after(act.activation(yT[b % 2][:], conv[:], ACT.Ln, bias=1.0))
            square_half(b, 0)

        def square_half(b, half):
            wait(act, got("part", b, 0) if half else None)
            ev["square", b, half] = S["act"].after(act.activation(
                hT[:], conv[:, half * PAIRS:(half + 1) * PAIRS, :], ACT.Square, scale=3.0 ** -0.5, bias=series_bias[:]))

        def softplus_relu(b):
            for pair in range(PAIRS):
                bank = ev["dt_bank", b, pair]
                wait(dve, ev["abs", b, pair], got("dA_all", b - 2), got("u", b - 2))
                for j in range(2):
                    m = 2 * pair + j
                    ev["relu", b] = freed[bank] = S["dve"].after(dve.tensor_scalar(
                        dt[b % 2][:, m, :], work[:, bank, j * L:(j + 1) * L], b_dt[:, m:m + 1], 0.0, ALU.add, ALU.max))

        def softplus_series(b, half):
            tiles = slice(half * PAIRS, (half + 1) * PAIRS)
            wait(dve, ev["square", b, half])
            e = S["dve"].after(dve.scalar_tensor_tensor(
                out=hT[:], in0=hT[:], scalar=13.0 / 16.0, in1=conv[:, tiles, :], op0=ALU.add, op1=ALU.mult))
            wait(dve, e, ev["relu", b])
            ev["part", b, half] = S["dve"].after(dve.scalar_tensor_tensor(
                out=dt[b % 2][:, tiles, :], in0=hT[:], scalar=LOG1P_SMALL * (LOG1P_SMALL ** 2 / 3 - LOG1P_SMALL / 2 + 1),
                in1=dt[b % 2][:, tiles, :], op0=ALU.min, op1=ALU.add))

        def softplus_sum(b):
            wait(dve, ev["log", b])
            e = S["dve"].after(dve.tensor_scalar(yT[b % 2][:], yT[b % 2][:], log_small[:], 0.0, ALU.subtract, ALU.max))
            wait(dve, e, ev["part", b, 1])
            ev["dt", b] = S["dve"].after(dve.tensor_tensor(dt[b % 2][:], dt[b % 2][:], yT[b % 2][:], ALU.add))

        def skip(b):
            wait(dve, got("dt", b))
            for m in range(M):
                ev["skip", b] = S["dve"].after(dve.tensor_scalar(
                    yT[b % 2][:, m, :], xs[b % 2][:, m, :], d_skip[:, m:m + 1], None, ALU.mult))

        def scale_x(b):
            wait(pool, got("skip", b), got("xd_ps", b))
            ev["u", b] = S["pool"].after(pool.tensor_tensor(xs[b % 2][:], xs[b % 2][:], dt[b % 2][:], ALU.mult))

        def chunk(b, c):
            pair, q = c // 4, c % 4
            g = b * SLOTS + c
            da, h = dA[g % DA], hs[g % 3]
            wait(act, got("dt", b), got("scan", g - DA))
            for j in range(2):
                m = 2 * pair + j
                for n in range(Q):
                    ev["dA", g] = ev["dA_all", b] = S["dA"].after(act.activation(
                        da[:, j, n, 1:L], dt[b % 2][:, m, 1:L], ACT.Exp, scale=a_neg[:, m, q * Q + n:q * Q + n + 1]))
            spread = lambda mat: mat[:].unsqueeze(1).broadcast_to([P, 2, Q, L])
            wait(pool, got("u", b), got("bc", b, q), got("y_ps", g - 3))
            ev["dbx", g] = ev["dbx_all", b] = S["dbx"].after(pool.tensor_tensor(
                h[:], xs[b % 2][:, 2 * pair:2 * pair + 2, :].unsqueeze(2).broadcast_to([P, 2, Q, L]),
                spread(bmat[q]), ALU.mult))
            flat = h[:].rearrange("p j n l -> p (j n l)")
            wait(dve, ev["dA", g], ev["dbx", g])
            ev["scan", g] = S["scan"].after(dve.tensor_tensor_scan(
                flat, da[:].rearrange("p j n l -> p (j n l)"), flat, 0.0, ALU.mult, ALU.add))
            wait(dve, ev["scan", g], got("bc", b, q))
            ev["hc", g] = S["hc"].after(dve.tensor_tensor(h[:], h[:], spread(cmat[q]), ALU.mult))

        def sum_states(g):
            turn_of, q = g // 4, g % 4
            wait(pe, got("hc", g), got("y", turn_of - 2) if q == 0 else None)
            for n in range(Q):
                mm = pe.matmul(yps[:, turn_of % 2, 0:2 * L], ident[:], hs[g % 3][:, :, n, :],
                               start=(q == 0 and n == 0), stop=(q == 3 and n == Q - 1))
            ev["y_ps", g] = S["y_ps"].after(mm)

        def add_y(b, pair):
            turn_of = b * PAIRS + pair
            dst = yT[b % 2][:, 2 * pair:2 * pair + 2, :]
            wait(dve, got("y_ps", 4 * turn_of + 3), got("skip", b))
            ev["y", turn_of] = S["evac"].after(dve.tensor_tensor(
                dst, dst, yps[:, turn_of % 2, 0:2 * L].rearrange("p (j l) -> p j l", j=2), ALU.add))

        def gate(b):
            wait(pool, got("y", b * PAIRS + PAIRS - 1), got("zs", b))
            ev["gated", b] = S["pool"].after(pool.tensor_tensor(yT[b % 2][:], yT[b % 2][:], zs[b % 2][:], ALU.mult))

        def out_proj(b, i, part):
            wait(pe, got("gated", b), w_out_loaded)
            bank = ev["o_bank", b, i] = ev["o_bank", b, i] if part else next_bank()
            for m in range(part * PAIRS, (part + 1) * PAIRS):
                mm = pe.matmul(work[0:TT, bank, :], yT[b % 2][:, m, i * TT:(i + 1) * TT], w_out[:, m, :],
                               start=(m == 0), stop=(m == M - 1))
            if part:
                ev["o_ps", b, i] = ev["o_ps", b] = S["work"].after(mm)

        def add_residual(b, i):
            bank = ev["o_bank", b, i]
            wait(dve, got("o_ps", b, i), got("res", b))
            e = freed[bank] = S["dve"].after(
                dve.tensor_tensor(xt[b % 3][:, i, :], xt[b % 3][:, i, :], work[0:TT, bank, :], ALU.add))
            wait(dve, e)
            e = S["dve"].after(dve.bn_stats(stats1[:, i, :], xt[b % 3][:, i, :]))
            wait(dve, e)
            e = S["dve"].after(dve.bn_aggr(mv1[:, 2 * b + i, :], stats1[:, i, :]))
            if i == 0:
                return
            ev["x1", b] = e
            wait(sp, e)
            ev["x1_stored", b] = S[f"xout{b % 3}"].after(
                sp.dma_start(x1_dram[b].rearrange("(i p) d -> p i d", p=TT), xt[b % 3][:]), 16)

        pieces = [w[r * P:(r + 1) * P, c * D:(c + 1) * D] for w in (t["w1"], t["w2"])
                  for r in range(w.shape[0] // P) for c in range(w.shape[1] // D)]
        assert len(pieces) <= B * SLOTS

        def load_piece(n):
            wait(sp, got("wsum", n - 2))
            ev["piece", n] = S[f"piece{n % 2}"].after(sp.dma_start(piece[n % 2][:], pieces[n]), 16)

        def sum_piece(n):
            wait(act, got("piece", n))
            ev["wsum", n] = S["act"].after(act.activation(
                piece[n % 2][:], piece[n % 2][:], ACT.Abs, accum_out=wsum[:, n:n + 1]))

        def load_kv():
            wait(sp, got("z_ps", B - 1, PAIRS - 1))
            for name, raw in (("Wk", shared.raw_k), ("Wv", shared.raw_v)):
                ev[name] = S[name.lower()].after(
                    sp.dma_start(raw[:], t[name].rearrange("(k p) d -> p k d", p=P)), 16)

        def split_kv(name, raw, parts):
            hi, lo = parts
            wait(dve, ev[name])
            e = S["split"].after(dve.tensor_copy(hi[:], raw[:]))
            wait(pool, e)
            S["pool"].after(pool.tensor_tensor(lo[:], raw[:], hi[:].bitcast(F32), ALU.subtract))

        steps = [
            (-24, lambda b: load_x(b) if b else None), (-23, row_stats), (-21, guess_rsqrt), (-21, normalise), (-20, transpose_h), (-19, scale_hT),
            *((p - 18, lambda b, p=p: project(b, "x_ps", p)) for p in range(PAIRS)),
            *((p - 16, lambda b, p=p: last_tap(b, p)) for p in range(PAIRS)),
            *((p - 16, lambda b, p=p: older_taps(b, p)) for p in range(PAIRS)),
            *((p - 14, lambda b, p=p: project(b, "z_ps", p)) for p in range(PAIRS)),
            *((p - 12, lambda b, p=p: keep_z(b, p)) for p in range(PAIRS)),
            (-9, silus), (-9, x_dbl), (-8, keep_xd), (-7, dt_raw),
            (-5, softplus_tables), (-5, softplus_relu), (-5, lambda b: softplus_series(b, 0)), (-3, lambda b: square_half(b, 1)),
            (-3, lambda b: softplus_series(b, 1)), (-3, softplus_sum), (-3, skip), (-1, scale_x),
            *((q - 3, lambda b, q=q: spread_bc(b, q)) for q in range(4)),
            (SLOTS + 2, gate),
            *((SLOTS + 4 + 2 * i + part, lambda b, i=i, part=part: out_proj(b, i, part))
              for i in range(2) for part in range(2)),
            *((SLOTS + 6 + 2 * i, lambda b, i=i: add_residual(b, i)) for i in range(2)),
        ]
        for slot in range(-24, B * SLOTS + SLOTS):
            for b in range(B):
                at = slot - b * SLOTS
                if 1 <= at <= SLOTS:
                    sum_states(b * SLOTS + at - 1)
                if 0 <= at < SLOTS:
                    chunk(b, at)
                if 5 <= at <= SLOTS + 1 and at % 4 == 1:
                    add_y(b, (at - 5) // 4)
            for b in range(B):
                for offset, step in steps:
                    if slot - b * SLOTS == offset:
                        step(b)
            if slot == (B - 1) * SLOTS:
                load_kv()
            if slot == B * SLOTS + 3:
                split_kv("Wk", shared.raw_k, shared.k)
            if slot == B * SLOTS + 4:
                split_kv("Wv", shared.raw_v, shared.v)
            if slot >= 0:
                every = B * SLOTS // len(pieces)
                n = slot // every
                if n < len(pieces) and slot % every == 0:
                    load_piece(n)
                if n < len(pieces) and slot % every == every - 1:
                    sum_piece(n)
        for b in range(B - 3, B):
            wait(sp, ev["x1_stored", b])
        nc.all_engine_barrier()




def rstd_of_rows(nc, mem, mv, rstd, done_act, done_dve):
    rows, tiles, _ = mv.shape
    var_eps, guess, tmp = (mem.sbuf(n, [rows, tiles]) for n in ("row_var", "row_guess", "row_tmp"))
    e = done_dve.after(nc.vector.tensor_scalar(var_eps[:], mv[:, :, 1], EPS, None, ALU.add))
    wait(nc.scalar, e)
    wait(nc.scalar, done_act.after(nc.scalar.activation(guess[:], var_eps[:], ACT.Ln)))
    e = done_act.after(nc.scalar.activation(guess[:], guess[:], ACT.Exp, scale=-0.5))
    wait(nc.vector, e)
    return newton_rsqrt(nc.vector, done_dve, rstd[:], guess[:], var_eps[:], tmp[:])


def attention_phase(nc, t, x1_dram, x2_dram, mv1, mv2, shared):
    B, D, KEYS = t["ctxT"].shape
    L = x1_dram.shape[1]
    TT = L // 2
    KD = D // P
    HEADS = 16
    DH = D // HEADS
    GROUP = P // DH
    GROUPS = HEADS // GROUP
    SLOTS = HEADS
    KC = 125
    CHUNKS = KEYS // KC
    HALF = KEYS // 2
    HPAD = HALF + HALF % 2
    KPAD = 2 * HPAD
    PAIRS = CHUNKS // 2
    RING = GROUP + 1
    RAWS = 4
    SCALE = float(DH) ** -0.5
    assert KC * CHUNKS == KEYS and CHUNKS % 2 == 0 and 2 * L <= BANK and HPAD <= BANK

    pe, act, dve, pool, sp = nc.tensor, nc.scalar, nc.vector, nc.gpsimd, nc.sync
    with ExitStack() as stack:
        mem = Memory(nc, stack, "b_")
        wk, wv = shared.k, shared.v
        wq = mem.sbuf("wq", [P, KD, D])
        wo = mem.sbuf("wo", [P, KD, D])
        bq = mem.sbuf("bq", [P, KD])
        bk = mem.sbuf("bk", [P, KD])
        bv = mem.sbuf("bv", [P, D])
        bo = mem.sbuf("bo", [P, D])
        ident = mem.sbuf("ident", [P, P])
        mask = mem.sbuf("mask", [TT, 2, KEYS])
        rstd = mem.sbuf("rstd", [TT, 2 * B])
        raw = [mem.sbuf(f"raw{i}", [P, KPAD]) for i in range(RAWS)]
        ctx = [mem.sbuf(f"ctx_{n}", [P, KD, KPAD], F32R) for n in ("hi", "lo")]
        k32 = [mem.sbuf(f"k32_{i}", [P, KPAD]) for i in range(2)]
        q32 = [mem.sbuf(f"q32_{i}", [P, L]) for i in range(2)]
        k_stack = [mem.sbuf(f"k_stack{j}", [P, KPAD], F32R) for j in range(GROUP)]
        q_stack = [mem.sbuf(f"q_stack{j}", [P, L], F32R) for j in range(GROUP)]
        v = [mem.sbuf(f"v{i}", [KC, CHUNKS, D]) for i in range(2)]
        xt = [mem.sbuf(f"xt{i}", [TT, 2, D]) for i in range(2)]
        ln = mem.sbuf("ln", [TT, 2, D])
        stats = mem.sbuf("stats", [TT, 2, 6])
        hT = mem.sbuf("hT", [P, KD, L])
        sc = [mem.sbuf(f"sc{i}", [TT, 2, KEYS]) for i in range(2)]
        nmax = mem.sbuf("nmax", [TT, 2, HEADS])
        esum = mem.sbuf("esum", [TT, 2, HEADS])
        rsum = mem.sbuf("rsum", [TT, 2, GROUP])
        rwide = mem.sbuf("rwide", [TT, 2, GROUP, DH])
        pT = [mem.sbuf(f"pT{i}", [KC, CHUNKS, L]) for i in range(RING)]
        rb = mem.sbuf("rb", [P, L])
        oT = [mem.sbuf(f"oT{i}", [P, GROUPS, L]) for i in range(2)]
        sps = mem.psum("sps", [P, 4, BANK])
        tps = mem.psum("tps", [P, 2, BANK])
        ups = mem.psum("ups", [P, 2, BANK])

        S = {n: mem.semaphore(n) for n in (
            "w", "wq", "rows", "mask", "wo", "w1", *(f"raw{i}" for i in range(RAWS)), "xin0", "xin1", "xout0", "xout1", "const", "act", "dve", "pool",
            "unit", "s_ps", "ttr", "exp", "t_ps", "pt_act", "pt_dve", "pv", "ctx_hi", "ctx_lo", "k_hi", "k_again",
            "k_lo", "q_hi", "q_lo", "free_act", "free_dve")}
        ev = {}

        def got(*key):
            assert key in ev or min(key[1:]) < 0, key
            return ev.get(key)

        for tile in raw:
            pads = S["const"].after(dve.memset(tile[:, KEYS:KPAD], 0.0))
        for dst, src in ((ident[:], t["ident"]), (bq[:], t["bq"]), (bk[:], t["bk"])):
            weights = S["w"].after(act.dma_start(dst, src), 16)
        wq_loaded = S["wq"].after(act.dma_start(wq[:], t["Wq"].rearrange("(k p) n -> p k n", p=P)), 16)
        for dst, src in ((bv[:], t["bv"].partition_broadcast(P)), (bo[:], t["bo"].partition_broadcast(P))):
            rows_loaded = S["rows"].after(act.dma_start(dst, src), 16)
        rstd_ready = rstd_of_rows(nc, mem, mv1, rstd, S["act"], S["dve"])
        for engine in (pe, act, dve):
            wait(engine, weights)
        wait(sp, pads)
        TERMS = ((0, 0), (0, 1), (1, 0))

        pool_last = [None]

        def load_x1(b):
            wait(sp, got("x2_stored", b - 2), got("x2_read", b - 2))
            ev["x1", b] = S[f"xin{b % 2}"].after(
                sp.dma_start(xt[b % 2][:], x1_dram[b].rearrange("(i p) d -> p i d", p=TT)), 16)

        def normalise(b):
            wait(dve, got("x1", b), got("hT_ps", b - 1, 1), rstd_ready)
            for i in range(2):
                ev["ln", b] = S["dve"].after(dve.tensor_scalar(
                    ln[:, i, :], xt[b % 2][:, i, :], mv1[:, 2 * b + i, 0:1], rstd[:, 2 * b + i:2 * b + i + 1],
                    ALU.subtract, ALU.mult))
            wait(pool, ev["ln", b], pool_last[0], rows_loaded)
            for i in range(2):
                pool_last[0] = ev["res", b] = S["pool"].after(pool.tensor_tensor(xt[b % 2][:, i, :], xt[b % 2][:, i, :], bo[0:TT, :], ALU.add))

        units = [0]
        freed = [None, None]

        def next_bank():
            bank = units[0] % 2
            units[0] += 1
            wait(pe, freed[bank])
            return bank

        def transpose_h(b, part):
            bank = next_bank()
            wait(pe, got("ln", b))
            for k2 in range(2):
                for i in range(2):
                    mm = pe.transpose(ups[:, bank, k2 * L + i * TT:k2 * L + (i + 1) * TT],
                                      ln[:, i, (2 * part + k2) * P:(2 * part + k2 + 1) * P], ident[0:TT, 0:TT])
            ev["hT_ps", b, part] = S["unit"].after(mm)
            wait(act, ev["hT_ps", b, part], got("q_ps", b - 1, GROUPS - 1))
            ev["hT", b] = freed[bank] = S["free_act"].after(act.activation(
                hT[:, 2 * part:2 * part + 2, :], ups[:, bank, 0:2 * L].rearrange("p (k l) -> p k l", k=2), ACT.Copy))

        def load_ctx(b, k):
            n = b * KD + k
            wait(sp, got("ctx_lo", n - RAWS))
            ev["raw", n] = S[f"raw{n % RAWS}"].after(
                sp.dma_start(raw[n % RAWS][:, 0:KEYS], t["ctxT"][b].rearrange("(k p) s -> p k s", p=P)[:, k, :]), 16)

        def split_ctx(b, k):
            n = b * KD + k
            stage = raw[n % RAWS]
            used = (got("k_ps", b - 1, GROUPS - 1, 1), got("v_ps", b - 1, CHUNKS - 1))
            wait(dve, ev["raw", n], *used)
            ev["ctx_hi", n] = S["ctx_hi"].after(dve.tensor_copy(ctx[0][:, k, :], stage[:]))
            wait(pool, ev["ctx_hi", n], *used, pool_last[0])
            pool_last[0] = ev["ctx_lo", n] = ev["ctx", b] = S["ctx_lo"].after(pool.tensor_tensor(
                ctx[1][:, k, :], stage[:], ctx[0][:, k, :].bitcast(F32), ALU.subtract))

        def project_k(b, g, half):
            G = b * GROUPS + g
            bank = next_bank()
            wait(pe, got("ctx", b))
            cols = slice(half * HPAD, (half + 1) * HPAD)
            for n, (i, j) in enumerate(TERMS):
                for k in range(KD):
                    mm = pe.matmul(ups[:, bank, 0:HPAD], wk[i][:, k, g * P:(g + 1) * P], ctx[j][:, k, cols],
                                   start=(n == 0 and k == 0), stop=(n == 2 and k == KD - 1))
            ev["k_ps", b, g, half] = S["unit"].after(mm)
            used = GROUP * (G - 1) - 1
            wait(act, ev["k_ps", b, g, half], got("k_lo", used), got("k_hi", used), got("k_again", used))
            ev["k32", G] = freed[bank] = S["free_act"].after(act.activation(
                k32[G % 2][:, cols], ups[:, bank, 0:HPAD], ACT.Identity, bias=bk[:, g:g + 1]))

        def project_v(b, c):
            bank = next_bank()
            wait(pe, got("ctx", b))
            for n, (i, j) in enumerate(TERMS):
                for k in range(KD):
                    mm = pe.matmul(ups[0:KC, bank, :], ctx[i][:, k, c * KC:(c + 1) * KC], wv[j][:, k, :],
                                   start=(n == 0 and k == 0), stop=(n == 2 and k == KD - 1))
            ev["v_ps", b, c] = S["unit"].after(mm)
            wait(dve, ev["v_ps", b, c], rows_loaded, got("pv", b - 2, GROUPS - 1))
            ev["v", b] = freed[bank] = S["free_dve"].after(
                dve.tensor_tensor(v[b % 2][:, c, :], ups[0:KC, bank, :], bv[0:KC, :], ALU.add))

        def project_q(b, g):
            G = b * GROUPS + g
            bank = next_bank()
            wait(pe, got("hT", b), wq_loaded)
            for k in range(KD):
                mm = pe.matmul(ups[:, bank, 0:L], wq[:, k, g * P:(g + 1) * P], hT[:, k, :],
                               start=(k == 0), stop=(k == KD - 1))
            ev["q_ps", b, g] = S["unit"].after(mm)
            used = GROUP * (G - 1) - 1
            wait(act, ev["q_ps", b, g], ev["bq"], got("q_lo", used), got("q_hi", used))
            ev["q32", G] = freed[bank] = S["free_act"].after(act.activation(
                q32[G % 2][:], ups[:, bank, 0:L], ACT.Identity, bias=bq[:, g:g + 1], scale=SCALE))

        def quadrant(n, turn):
            start = (n + turn) % GROUP * DH
            return slice(start, start + DH)

        def stack_head(n):
            G = n // GROUP
            ks, qs, k, q = k_stack[n % GROUP], q_stack[n % GROUP], k32[G % 2], q32[G % 2]
            rows = quadrant(n, 0)
            used = got("s_ps", n - GROUP)
            wait(dve, ev["k32", G], used)
            e = ev["k_hi", n] = S["k_hi"].after(dve.tensor_copy(ks[rows, :], k[rows, :]))
            wait(pool, e, used, pool_last[0])
            pool_last[0] = ev["k_lo", n] = S["k_lo"].after(pool.tensor_tensor(
                ks[quadrant(n, 1), :], k[rows, :], ks[rows, :].bitcast(F32), ALU.subtract))
            wait(dve, ev["q32", G])
            e = S["q_hi"].after(dve.tensor_copy(qs[rows, :], q[rows, :]))
            ev["q_hi", n] = S["q_hi"].after(dve.tensor_copy(qs[quadrant(n, 1), :], q[rows, :]))
            wait(dve, e)
            ev["q_lo", n] = S["q_lo"].after(dve.tensor_tensor(
                qs[quadrant(n, 2), :], q[rows, :], qs[rows, :].bitcast(F32), ALU.subtract))

        def stack_k_again(n):
            G = n // GROUP
            wait(act, ev["k32", G], got("s_ps", n - GROUP))
            ev["k_again", n] = S["k_again"].after(act.activation(
                k_stack[n % GROUP][quadrant(n, 2), :], k32[G % 2][quadrant(n, 0), :], ACT.Copy))

        def scores(n):
            wait(pe, got("k_hi", n), got("k_lo", n), got("k_again", n), got("q_hi", n), got("q_lo", n))
            for i in range(2):
                wait(pe, got("ttr", n - 1, i))
                for half in range(2):
                    mm = pe.matmul(sps[0:TT, 2 * i + half, 0:HPAD], q_stack[n % GROUP][:, i * TT:(i + 1) * TT],
                                   k_stack[n % GROUP][:, half * HALF:half * HALF + HPAD], start=True, stop=True)
                ev["s_ps", n, i] = ev["s_ps", n] = S["s_ps"].after(mm)

        def load_late():
            ev["mask_loaded"] = S["mask"].after(act.dma_start(mask[:], t["mask"].rearrange("(i p) k -> p i k", p=TT)), 16)
            ev["wo"] = S["wo"].after(act.dma_start(wo[:], t["Wo"].rearrange("(k p) n -> p k n", p=P)), 16)

        def clear_stacks():
            for tile in (*k_stack, *q_stack):
                stacks = S["const"].after(dve.memset(tile[:].bitcast(F32), 0.0))
            for engine in (act, dve, pool):
                wait(engine, stacks)

        def scale_bq():
            ev["bq"] = S["const"].after(dve.tensor_scalar(bq[:], bq[:], SCALE, None, ALU.mult))

        def scale_mask():
            wait(dve, ev["mask_loaded"])
            ev["mask"] = S["const"].after(dve.tensor_scalar(mask[:], mask[:], NEG_INF_SCALE, None, ALU.mult))

        def negate_and_mask(n):
            h = n % HEADS
            for i in range(2):
                wait(dve, got("s_ps", n, i), got("t_ps", n - 2, PAIRS - 1), ev["mask"])
                ev["ttr", n, i] = S["ttr"].after(dve.tensor_tensor_reduce(
                    out=sc[n % 2][:, i, :].rearrange("p (a k) -> p a k", a=2), in0=sps[0:TT, 2 * i:2 * i + 2, 0:HALF],
                    in1=mask[:, i, :].rearrange("p (a k) -> p a k", a=2), scale=-1.0, scalar=3.0e38,
                    op0=ALU.add, op1=ALU.min, accum_out=nmax[:, i, h:h + 1]))

        def exponentials(n):
            h = n % HEADS
            for i in range(2):
                wait(act, ev["ttr", n, i], got("rsum", n // GROUP - GROUPS))
                ev["exp", n] = S["exp"].after(act.activation(
                    sc[n % 2][:, i, :], sc[n % 2][:, i, :], ACT.Exp, scale=-1.0, bias=nmax[:, i, h:h + 1],
                    accum_out=esum[:, i, h:h + 1]))

        def transpose_p(n, pair, engine):
            tile = n * PAIRS + pair
            bank = tile % 2
            wait(pe, got("exp", n), got("t_free", tile - 2))
            for c2 in range(2):
                c = 2 * pair + c2
                for i in range(2):
                    mm = pe.transpose(tps[0:KC, bank, c2 * L + i * TT:c2 * L + (i + 1) * TT],
                                      sc[n % 2][:, i, c * KC:(c + 1) * KC], ident[0:TT, 0:TT])
            e = ev["t_ps", n, pair] = S["t_ps"].after(mm)
            dst = pT[n % RING][:, 2 * pair:2 * pair + 2, :]
            src = tps[0:KC, bank, 0:2 * L].rearrange("p (c l) -> p c l", c=2)
            G = (n - RING) // GROUP
            wait(engine, e, got("pv", G // GROUPS, G % GROUPS) if n >= RING else None)
            if engine is act:
                ev["t_free", tile] = ev["pT_act", n] = S["pt_act"].after(act.activation(dst, src, ACT.Copy))
            else:
                ev["t_free", tile] = ev["pT_dve", n] = S["pt_dve"].after(dve.tensor_copy(dst, src))

        def invert_sums(b, g):
            G = b * GROUPS + g
            wait(dve, got("exp", G * GROUP + GROUP - 1), got("r_ps", G - 1))
            e = ev["rsum", G] = S["dve"].after(dve.reciprocal(rsum[:], esum[:, :, g * GROUP:(g + 1) * GROUP]))
            wait(dve, e)
            for i in range(2):
                ev["rwide", G] = S["dve"].after(
                    dve.tensor_copy(rwide[:, i], rsum[:, i, :].unsqueeze(2).broadcast_to([TT, GROUP, DH])))

        def spread_sums(b, g):
            G = b * GROUPS + g
            bank = next_bank()
            wait(pe, got("rwide", G))
            for i in range(2):
                mm = pe.matmul(ups[:, bank, i * TT:(i + 1) * TT], rwide[:, i].rearrange("p j d -> p (j d)"),
                               ident[0:TT, 0:TT], start=True, stop=True)
            ev["r_ps", G] = S["unit"].after(mm)
            wait(act, ev["r_ps", G], got("oT", G - 1))
            ev["rb", G] = freed[bank] = S["free_act"].after(act.activation(rb[:], ups[:, bank, 0:L], ACT.Copy))

        def weigh_v(b, g):
            G = b * GROUPS + g
            last = G * GROUP + GROUP - 1
            bank = ev["pv_bank", G] = next_bank()
            wait(pe, got("pT_act", last), got("pT_dve", last), got("v", b))
            for c in range(CHUNKS):
                for j in range(GROUP):
                    mm = pe.matmul(ups[j * DH:(j + 1) * DH, bank, 0:L],
                                   v[b % 2][:, c, (g * GROUP + j) * DH:(g * GROUP + j + 1) * DH],
                                   pT[(G * GROUP + j) % RING][:, c, :], start=(c == 0), stop=(c == CHUNKS - 1))
            ev["pv", b, g] = S["pv"].after(mm)

        def scale_o(b, g):
            G = b * GROUPS + g
            bank = ev["pv_bank", G]
            wait(dve, got("pv", b, g), got("rb", G), got("o_ps", b - 2))
            ev["oT", G] = freed[bank] = S["free_dve"].after(
                dve.tensor_tensor(oT[b % 2][:, g, :], ups[:, bank, 0:L], rb[:], ALU.mult))

        def out_proj(b, i):
            bank = next_bank()
            wait(pe, got("oT", b * GROUPS + GROUPS - 1), ev["wo"])
            for g in range(GROUPS):
                mm = pe.matmul(ups[0:TT, bank, :], oT[b % 2][:, g, i * TT:(i + 1) * TT], wo[:, g, :],
                               start=(g == 0), stop=(g == GROUPS - 1))
            ev["o_ps", b] = S["unit"].after(mm)
            wait(dve, ev["o_ps", b], got("res", b))
            ev["x2", b, i] = freed[bank] = S["free_dve"].after(
                dve.tensor_tensor(xt[b % 2][:, i, :], xt[b % 2][:, i, :], ups[0:TT, bank, :], ALU.add))

        def row_stats(b):
            wait(dve, ev["x2", b, 1])
            for i in range(2):
                e = S["dve"].after(dve.bn_stats(stats[:, i, :], xt[b % 2][:, i, :]))
            ev["x2_read", b] = e
            wait(dve, e)
            for i in range(2):
                S["dve"].after(dve.bn_aggr(mv2[:, 2 * b + i, :], stats[:, i, :]))
            wait(sp, ev["x2", b, 1])
            ev["x2_stored", b] = S[f"xout{b % 2}"].after(
                sp.dma_start(x2_dram[b].rearrange("(i p) d -> p i d", p=TT), xt[b % 2][:]), 16)

        def load_w1():
            wait(sp, got("k_ps", B - 1, GROUPS - 1, 1), got("v_ps", B - 1, CHUNKS - 1))
            ev["w1"] = S["w1"].after(sp.dma_start(shared.raw_1[:], t["w1T"].rearrange("(k p) f -> p k f", p=P)), 16)

        def sign_w1(k):
            wait(act, ev["w1"])
            S["act"].after(act.activation(shared.s1[:, k, :], shared.raw_1[:, k, :], ACT.Sign))

        scaled = [(4 * g + 6, lambda b, g=g: scale_o(b, g)) for g in range(GROUPS)]
        early = [
            (-13, lambda b: load_ctx(b, 0)), (-13, lambda b: load_ctx(b, 1)),
            (-12, lambda b: load_ctx(b, 2)), (-12, lambda b: load_ctx(b, 3)),
            (-8, lambda b: split_ctx(b, 0)), (-8, lambda b: split_ctx(b, 1)),
            (-7, lambda b: split_ctx(b, 2)), (-7, lambda b: split_ctx(b, 3)),
            (-8, load_x1), (-6, normalise),
            *((4 * g + 5, lambda b, g=g: invert_sums(b, g)) for g in range(GROUPS)),
            (SLOTS + 8, row_stats),
        ]
        first = [
            *((4 * g - 6, lambda b, g=g: project_k(b, g, 0)) for g in range(GROUPS)),
            *((4 * g - 5, lambda b, g=g: project_k(b, g, 1)) for g in range(GROUPS)),
            *((4 * g - 4, lambda b, g=g: project_q(b, g)) for g in range(GROUPS)),
            *((4 * g + 5, lambda b, g=g: weigh_v(b, g)) for g in range(GROUPS)),
        ]
        second = [
            (-5, lambda b: transpose_h(b, 0)), (-5, lambda b: transpose_h(b, 1)),
            *((slot, lambda b, c=c: project_v(b, c)) for c, slot in enumerate((-4, -2, -1, 0, 2, 3))),
            *((4 * g + 5, lambda b, g=g: spread_sums(b, g)) for g in range(GROUPS)),
            (SLOTS + 4, lambda b: out_proj(b, 0)), (SLOTS + 7, lambda b: out_proj(b, 1)),
        ]

        def issue(steps, slot):
            for b in range(B):
                for offset, step in steps:
                    if slot - b * SLOTS == offset:
                        step(b)

        for slot in range(early[0][0], B * SLOTS + SLOTS // 2 + 1):
            now = 0 <= slot < B * SLOTS
            if slot == -6:
                scale_bq()
                load_late()
                clear_stacks()
            if slot == -1:
                scale_mask()
            if slot == B * SLOTS - 6:
                load_w1()
            if slot - B * SLOTS - 3 in range(KD):
                sign_w1(slot - B * SLOTS - 3)
            before = 1 <= slot <= B * SLOTS
            if now:
                scores(slot)
            issue(scaled, slot)
            if now:
                negate_and_mask(slot)
            issue(early, slot)
            if before:
                transpose_p(slot - 1, 0, act)
            if now:
                exponentials(slot)
            if 0 <= slot + 2 < B * SLOTS:
                stack_head(slot + 2)
            issue(first, slot)
            if before:
                transpose_p(slot - 1, 1, dve)
            if 0 <= slot + 2 < B * SLOTS:
                stack_k_again(slot + 2)
            issue(second, slot)
            if before:
                transpose_p(slot - 1, 2, act)
        for b in range(B - 2, B):
            wait(sp, ev["x2_stored", b])
        nc.all_engine_barrier()


def ffn_phase(nc, t, x2_dram, out, mv2, wsum, shared):
    B, L, D = x2_dram.shape
    TT = L // 2
    TILES = 4
    T = TILES * TT
    STEPS = B * L // T
    KD = D // P
    F = t["w1"].shape[0]
    FT = F // P
    LAG = 2
    assert T <= BANK and D <= BANK and wsum.shape[1] == FT + F // D * KD

    pe, act, dve, pool, sp = nc.tensor, nc.scalar, nc.vector, nc.gpsimd, nc.sync
    with ExitStack() as stack:
        mem = Memory(nc, stack, "c_")
        s1 = shared.s1
        place = mem.arena("w2", [P, FT, D])
        w2, s2 = mem.inside("raw_w2", [P, FT, D], place), mem.inside("s2", [P, FT, D], place, F32R)
        b1 = mem.sbuf("b1", [P, FT])
        b2 = mem.sbuf("b2", [P, D])
        ident = mem.sbuf("ident", [P, P])
        ones = mem.sbuf("ones", [P, P])
        alpha1 = mem.sbuf("alpha1", [P, FT])
        alpha2 = mem.sbuf("alpha2", [P, KD])
        diag = mem.sbuf("diag", [P, KD, P])
        alpha2_row = mem.sbuf("alpha2_row", [P, D])
        rstd = mem.sbuf("rstd", [TT, 2 * B])
        xt = [mem.sbuf(f"xt{i}", [TT, TILES, D]) for i in range(3)]
        ln = mem.sbuf("ln", [TT, TILES, D])
        hT = [[mem.sbuf(f"hT{i}_{n}", [P, KD, T], F32R) for n in ("hi", "lo")] for i in range(2)]
        g32 = [mem.sbuf(f"g32_{i}", [P, T]) for i in range(2)]
        gT = [[mem.sbuf(f"gT{i}_{n}", [P, T], F32R) for n in ("hi", "lo")] for i in range(LAG + 1)]
        prod = [mem.sbuf(f"prod{i}", [TT, D]) for i in range(2)]
        tps = mem.psum("tps", [P, BANK])
        fps = mem.psum("fps", [P, 3, BANK])
        ops = mem.psum("ops", [P, TILES, BANK])

        S = {n: mem.semaphore(n) for n in (
            "w", *(f"w2_{a}" for a in range(KD)), "xin0", "xin1", "xin2", "xout0", "xout1", "xout2", "const", "act", "dve",
            "sign", "pool", "t_ps", "h_hi", "h_lo", "f_ps", "gelu", "g_hi", "g_lo", "o_ps", "prod", "sum")}
        ev = {}

        def got(*key):
            assert key in ev or min(key[1:]) < 0, key
            return ev.get(key)

        for dst, src in ((b1[:], t["b1"]), (ident[:], t["ident"]), (b2[:], t["b2"].partition_broadcast(P))):
            weights = S["w"].after(act.dma_start(dst, src), 16)
        w2T = t["w2T"].rearrange("(a c p) d -> a p c d", p=P, c=F // D)
        quarter = [slice(a * (F // D), (a + 1) * (F // D)) for a in range(KD)]
        w2_loaded = [S[f"w2_{a}"].after(act.dma_start(w2[:, quarter[a], :], w2T[a]), 16) for a in range(KD)]
        rstd_ready = rstd_of_rows(nc, mem, mv2, rstd, S["act"], S["dve"])

        for engine in (dve, pe, act, pool):
            wait(engine, weights)
        alpha1_ready = S["const"].after(dve.tensor_scalar(alpha1[:], wsum[:, 0:FT], 1.0 / D, None, ALU.mult))
        e = S["const"].after(dve.tensor_reduce(
            alpha2[:], wsum[:, FT:].rearrange("p (r c) -> p r c", c=F // D), AX_X, ALU.add))
        wait(dve, e)
        for k in range(KD):
            S["const"].after(dve.tensor_scalar(diag[:, k, :], ident[:], alpha2[:, k:k + 1], 1.0 / F, ALU.mult, ALU.mult))
        e = S["const"].after(dve.memset(ones[:], 1.0))
        wait(pe, e)
        for k in range(KD):
            mm = pe.matmul(tps[:, k * P:(k + 1) * P], ones[:], diag[:, k, :], start=True, stop=True)
        e = S["t_ps"].after(mm)
        wait(dve, e)
        alpha2_ready = S["const"].after(dve.tensor_copy(alpha2_row[:], tps[:, 0:D]))
        wait(pe, alpha2_ready)
        wait(act, alpha1_ready)

        x2_tiles = x2_dram.rearrange("b (i p) d -> p (b i) d", p=TT)
        out_tiles = out.rearrange("b (i p) d -> p (b i) d", p=TT)

        def sign_w2(a):
            wait(act, w2_loaded[a])
            ev["sign", a] = S["sign"].after(act.activation(s2[:, quarter[a], :], w2[:, quarter[a], :], ACT.Sign))

        def load_x2(c):
            wait(sp, got("stored", c - 3))
            ev["x2", c] = S[f"xin{c % 3}"].after(
                sp.dma_start(xt[c % 3][:], x2_tiles[:, TILES * c:TILES * (c + 1), :]), 16)

        def normalise(c):
            wait(dve, got("x2", c), got("h_ps", c - 1, KD - 1), rstd_ready)
            for i in range(TILES):
                n = TILES * c + i
                ev["ln", c] = S["dve"].after(dve.tensor_scalar(
                    ln[:, i, :], xt[c % 3][:, i, :], mv2[:, n, 0:1], rstd[:, n:n + 1], ALU.subtract, ALU.mult))
            wait(pool, ev["ln", c])
            for i in range(TILES):
                ev["res", c] = S["pool"].after(pool.tensor_tensor(
                    xt[c % 3][:, i, :], xt[c % 3][:, i, :], b2[0:TT, :], ALU.add))

        def transpose_h(c, k):
            wait(pe, got("ln", c), got("h_lo", c, k - 1) if k else got("h_lo", c - 1, KD - 1))
            for i in range(TILES):
                mm = pe.transpose(tps[:, i * TT:(i + 1) * TT], ln[:, i, k * P:(k + 1) * P], ident[0:TT, 0:TT])
            ev["h_ps", c, k] = S["t_ps"].after(mm)
            hi, lo = hT[c % 2]
            used = got("f_ps", (c - 2) * FT + FT - 1)
            wait(act, ev["h_ps", c, k], used)
            e = S["h_hi"].after(act.activation(hi[:, k, :], tps[:, 0:T], ACT.Copy))
            wait(dve, e, used)
            ev["h_lo", c, k] = S["h_lo"].after(
                dve.tensor_tensor(lo[:, k, :], tps[:, 0:T], hi[:, k, :].bitcast(F32), ALU.subtract))

        def hidden(n):
            c, f = n // FT, n % FT
            wait(pe, got("h_lo", c, KD - 1), got("gelu", n - 3))
            for k in range(KD):
                for part in range(2):
                    mm = pe.matmul(fps[:, n % 3, 0:T], s1[:, k, f * P:(f + 1) * P], hT[c % 2][part][:, k, :],
                                   start=(k == 0 and part == 0), stop=(k == KD - 1 and part == 1))
            ev["f_ps", n] = S["f_ps"].after(mm)
            wait(act, ev["f_ps", n], got("g_lo", n - 2))
            ev["gelu", n] = S["gelu"].after(act.activation(
                g32[n % 2][:], fps[:, n % 3, 0:T], ACT.Gelu, scale=alpha1[:, f:f + 1], bias=b1[:, f:f + 1]))
            hi, lo = gT[n % (LAG + 1)]
            wait(dve, ev["gelu", n], got("o_ps", n - LAG - 1))
            e = S["g_hi"].after(dve.tensor_copy(hi[:], g32[n % 2][:]))
            wait(pool, e, got("o_ps", n - LAG - 1))
            ev["g_lo", n] = S["g_lo"].after(pool.tensor_tensor(lo[:], g32[n % 2][:], hi[:].bitcast(F32), ALU.subtract))

        def second(n):
            c, f = n // FT, n % FT
            wait(pe, got("g_lo", n), ev["sign", f // (F // D)])
            for i in range(TILES):
                if f == 0:
                    wait(pe, got("prod", c - 1, i))
                for part in range(2):
                    mm = pe.matmul(ops[0:TT, i, :], gT[n % (LAG + 1)][part][:, i * TT:(i + 1) * TT], s2[:, f, :],
                                   start=(f == 0 and part == 0), stop=(f == FT - 1 and part == 1))
                if f == FT - 1:
                    ev["o_tile", c, i] = S["o_ps"].after(mm)
            ev["o_ps", n] = S["o_ps"].after(mm) if f < FT - 1 else ev["o_tile", c, TILES - 1]

        def finish(c):
            for i in range(TILES):
                m = c * TILES + i
                wait(dve, ev["o_tile", c, i], got("sum", m - 2))
                ev["prod", c, i] = S["prod"].after(
                    dve.tensor_tensor(prod[m % 2][:], ops[0:TT, i, :], alpha2_row[0:TT, :], ALU.mult))
                wait(pool, ev["prod", c, i], got("res", c))
                ev["sum", m] = S["sum"].after(
                    pool.tensor_tensor(xt[c % 3][:, i, :], xt[c % 3][:, i, :], prod[m % 2][:], ALU.add))
            wait(sp, ev["sum", m])
            ev["stored", c] = S[f"xout{c % 3}"].after(
                sp.dma_start(out_tiles[:, TILES * c:TILES * (c + 1), :], xt[c % 3][:]), 16)

        steps = [(-12, load_x2), (-8, normalise), *((k - 6, lambda c, k=k: transpose_h(c, k)) for k in range(KD)),
                 (FT + LAG - 1, finish)]
        for slot in range(-12, STEPS * FT + LAG + 1):
            if slot + 1 in range(0, FT, F // D):
                sign_w2((slot + 1) // (F // D))
            if 0 <= slot < STEPS * FT:
                hidden(slot)
            if LAG <= slot < STEPS * FT + LAG:
                second(slot - LAG)
            for c in range(STEPS):
                for offset, step in steps:
                    if slot - c * FT == offset:
                        step(c)
        for c in range(STEPS - 3, STEPS):
            wait(sp, ev["stored", c])


def decoder_layer(nc, t, out):
    B, L, D = t["x"].shape
    TT = L // 2
    N = t["A_log"].shape[1]
    F = t["w1"].shape[0]
    x1_dram = nc.dram_tensor("x1_scratch", (B, L, D), F32).ap()
    x2_dram = nc.dram_tensor("x2_scratch", (B, L, D), F32).ap()
    bc_dram = nc.dram_tensor("bc_scratch", (B, 2 * N, L), F32).ap()
    with ExitStack() as stack:
        mem = Memory(nc, stack, "")
        mv1 = mem.sbuf("mv1", [TT, 2 * B, 2])
        mv2 = mem.sbuf("mv2", [TT, 2 * B, 2])
        wsum = mem.sbuf("wsum", [P, F // P + F // D * (D // P)])
        shared = Shared(mem, D, F)
        mamba_phase(nc, t, x1_dram, bc_dram, mv1, wsum, shared)
        attention_phase(nc, t, x1_dram, x2_dram, mv1, mv2, shared)
        ffn_phase(nc, t, x2_dram, out, mv2, wsum, shared)


def kernel(**inputs):
    import concourse.bacc as bacc
    from concourse.bass_utils import run_bass_kernel_spmd

    def columns(a):
        return np.asarray(a).reshape(-1, P).T

    i = {k: np.asarray(v) for k, v in inputs.items()}
    mamba = {k: i["L0_attn_" + k] for k in ("W_in", "conv_w", "W_x", "W_dt", "A_log", "W_out")}
    mamba |= {k: columns(i["L0_attn_" + k]) for k in ("norm_w", "conv_b", "b_dt", "D")}
    xattn = {k: i["L0_xattn_" + k] for k in ("Wq", "Wk", "Wv", "Wo", "bv", "bo")}
    xattn |= {k: columns(i["L0_xattn_" + k]) for k in ("bq", "bk")}
    ffn = {"w1": i["L0_ffn_w1"], "w2": i["L0_ffn_w2"], "w1T": i["L0_ffn_w1"].T, "w2T": i["L0_ffn_w2"].T,
           "b1": columns(i["L0_ffn_b1"]), "b2": i["L0_ffn_b2"]}
    arrays = {"x": i["x"], "ctxT": i["ctx_1024"].transpose(0, 2, 1), "mask": i["mask_1x1xSxS2_fk1"][0, 0],
              "ident": np.eye(P, dtype=np.float32), **mamba, **xattn, **ffn}
    arrays = {k: np.ascontiguousarray(a) for k, a in arrays.items()}

    nc = bacc.Bacc("TRN2", target_bir_lowering=False, num_devices=1)
    t = {k: nc.dram_tensor(k + "_dram", a.shape, mybir.dt.from_np(a.dtype), kind="ExternalInput").ap()
         for k, a in arrays.items()}
    out = nc.dram_tensor("out_dram", i["x"].shape, F32, kind="ExternalOutput").ap()
    decoder_layer(nc, t, out)
    result = run_bass_kernel_spmd(nc, [{k + "_dram": a for k, a in arrays.items()}], core_ids=[0])
    return result.results[0]["out_dram"]
```
